# Optimizing a Trainium2 kernel written in Bass

```python
import numpy as np
import jax
import jax.numpy as jnp

def _softmax(x, axis=-1):
    return jax.nn.softmax(x, axis=axis)

def _gelu(x):
    return jax.nn.gelu(x, approximate=True)

def _silu(x):
    return jax.nn.silu(x)

def _sigmoid(x):
    return jax.nn.sigmoid(x)

def _layernorm(x, axis=-1, eps=1e-05):
    m = jnp.mean(x, axis=axis, keepdims=True)
    v = jnp.var(x, axis=axis, keepdims=True)
    return (x - m) / jnp.sqrt(v + eps)

def _scatter_add(tgt, idx, src, axis=0):
    return tgt.at[idx].add(src)

def _segment_sum(src, seg, n):
    return jax.ops.segment_sum(src, seg, n)
kernel_name = 'mk_prb_d1_jaxref_r8_406f87'

def setup_inputs(seed: int=0):
    np.random.seed(seed)
    _w = jnp.asarray

    def _L0_attn_setup():
        import jax, jax.numpy as jnp
        import numpy as np
        D_MODEL = 128
        H = 16
        BZ = 64
        key = jax.random.key(seed)
        ks = jax.random.split(key, 9)
        B, N = (4, 512)
        s = 1.0 / np.sqrt(D_MODEL)
        x = jax.random.normal(ks[0], (B, N, D_MODEL), jnp.float32)
        Wq = jax.random.normal(ks[1], (D_MODEL, D_MODEL), jnp.float32) * s
        Wk = jax.random.normal(ks[2], (D_MODEL, D_MODEL), jnp.float32) * s
        Wv = jax.random.normal(ks[3], (D_MODEL, D_MODEL), jnp.float32) * s
        Wo = jax.random.normal(ks[4], (D_MODEL, D_MODEL), jnp.float32) * s
        bq = jax.random.normal(ks[5], (D_MODEL,), jnp.float32) * 0.01
        bk = jax.random.normal(ks[6], (D_MODEL,), jnp.float32) * 0.01
        bv = jax.random.normal(ks[7], (D_MODEL,), jnp.float32) * 0.01
        bo = jax.random.normal(ks[8], (D_MODEL,), jnp.float32) * 0.01
        return {'x': x, 'Wq': Wq, 'bq': bq, 'Wk': Wk, 'bk': bk, 'Wv': Wv, 'bv': bv, 'Wo': Wo, 'bo': bo}
    _L0_attn_in = _L0_attn_setup()

    def _L0_ffn_setup():
        import jax, jax.numpy as jnp
        import numpy as np
        BS, L, D = (4, 256, 128)
        H, E, K = (8, 16, 2)
        HD = D // H
        I = 512 // H
        key = jax.random.key(seed)
        ks = jax.random.split(key, 10)
        s = lambda k, shp, fan: jax.random.normal(k, shp, jnp.float32) / np.sqrt(fan)
        return {'x': jax.random.normal(ks[0], (BS, L, D), jnp.float32), 'Wm': s(ks[1], (D, D), D), 'bm': jnp.zeros((D,), jnp.float32), 'expert_emb': jax.random.normal(ks[2], (HD, E), jnp.float32), 'W1': s(ks[3], (E, HD, I), HD), 'b1': jnp.zeros((E, I), jnp.float32), 'W2': s(ks[4], (E, I, HD), I), 'b2': jnp.zeros((E, HD), jnp.float32), 'Wo': s(ks[5], (D, D), D), 'bo': jnp.zeros((D,), jnp.float32)}
    _L0_ffn_in = _L0_ffn_setup()
    _d = {'L0_attn_x': _L0_attn_in['x'], 'L0_attn_Wq': _L0_attn_in['Wq'], 'L0_attn_bq': _L0_attn_in['bq'], 'L0_attn_Wk': _L0_attn_in['Wk'], 'L0_attn_bk': _L0_attn_in['bk'], 'L0_attn_Wv': _L0_attn_in['Wv'], 'L0_attn_bv': _L0_attn_in['bv'], 'L0_attn_Wo': _L0_attn_in['Wo'], 'L0_attn_bo': _L0_attn_in['bo'], 'L0_ffn_Wm': _L0_ffn_in['Wm'], 'L0_ffn_bm': _L0_ffn_in['bm'], 'L0_ffn_expert_emb': _L0_ffn_in['expert_emb'], 'L0_ffn_W1': _L0_ffn_in['W1'], 'L0_ffn_b1': _L0_ffn_in['b1'], 'L0_ffn_W2': _L0_ffn_in['W2'], 'L0_ffn_b2': _L0_ffn_in['b2'], 'L0_ffn_Wo': _L0_ffn_in['Wo'], 'L0_ffn_bo': _L0_ffn_in['bo']}
    _x0 = _d['L0_attn_x']
    _d['L0_attn_x'] = jax.random.normal(jax.random.fold_in(jax.random.key(seed), 1), (16, 512, 128), dtype=_x0.dtype)
    del _x0
    return _d

def reference(L0_attn_x, L0_attn_Wq, L0_attn_bq, L0_attn_Wk, L0_attn_bk, L0_attn_Wv, L0_attn_bv, L0_attn_Wo, L0_attn_bo, L0_ffn_Wm, L0_ffn_bm, L0_ffn_expert_emb, L0_ffn_W1, L0_ffn_b1, L0_ffn_W2, L0_ffn_b2, L0_ffn_Wo, L0_ffn_bo):

    def _L0_attn_ref(x, Wq, bq, Wk, bk, Wv, bv, Wo, bo):
        import jax, jax.numpy as jnp
        import numpy as np
        D_MODEL = 128
        H = 16
        BZ = 64
        B, N, _ = x.shape
        Dh = D_MODEL // H
        nb = N // BZ
        scale = 1.0 / jnp.sqrt(jnp.asarray(Dh, x.dtype))
        q = (x @ Wq + bq).reshape(B, N, H, Dh).transpose(0, 2, 1, 3)
        k = (x @ Wk + bk).reshape(B, N, H, Dh).transpose(0, 2, 1, 3)
        v = (x @ Wv + bv).reshape(B, N, H, Dh).transpose(0, 2, 1, 3)
        qb = q.reshape(B, H, nb, BZ, Dh)
        kb = k.reshape(B, H, nb, BZ, Dh)
        vb = v.reshape(B, H, nb, BZ, Dh)
        att0 = jnp.einsum('bhqd,bhkd->bhqk', qb[:, :, 0], k) * scale
        out0 = jnp.einsum('bhqk,bhkd->bhqd', jax.nn.softmax(att0, axis=-1), v)
        bi = jnp.arange(1, nb)
        widx = jnp.stack([bi, bi - 1, jnp.minimum(bi + 1, nb - 1)], axis=1)
        kw = kb[:, :, widx]
        vw = vb[:, :, widx]
        ones = jnp.ones_like(bi, dtype=bool)
        valid = jnp.stack([ones, ones, bi + 1 <= nb - 1], axis=1)
        att = jnp.einsum('bhnqd,bhnwkd->bhnqwk', qb[:, :, 1:], kw) * scale
        att = jnp.where(valid[None, None, :, None, :, None], att, -jnp.inf)
        p = jax.nn.softmax(att.reshape(B, H, nb - 1, BZ, 3 * BZ), axis=-1)
        p = p.reshape(B, H, nb - 1, BZ, 3, BZ)
        outw = jnp.einsum('bhnqwk,bhnwkd->bhnqd', p, vw)
        out = jnp.concatenate([out0[:, :, None], outw], axis=2)
        out = out.reshape(B, H, N, Dh).transpose(0, 2, 1, 3).reshape(B, N, D_MODEL)
        return out @ Wo + bo

    def _L0_ffn_ref(x, Wm, bm, expert_emb, W1, b1, W2, b2, Wo, bo):
        import jax, jax.numpy as jnp
        import numpy as np
        BS, L, D = (4, 256, 128)
        H, E, K = (8, 16, 2)
        HD = D // H
        I = 512 // H
        bs, L_, d = x.shape
        h = x @ Wm + bm
        t = h.reshape(bs * L_ * H, HD)
        logits = t @ expert_emb
        w = jax.nn.softmax(logits, axis=-1)
        topw, topi = jax.lax.top_k(w, K)
        hmid = jax.nn.gelu(jnp.einsum('td,edi->tei', t, W1) + b1, approximate=False)
        eo = jnp.einsum('tei,eio->teo', hmid, W2) + b2
        sel = jnp.take_along_axis(eo, topi[:, :, None], axis=1)
        comb = (sel * topw[:, :, None]).sum(axis=1)
        out = comb.reshape(bs, L_, d)
        return out @ Wo + bo
    x = L0_attn_x
    xn = _layernorm(x, axis=-1)
    x = x + _L0_attn_ref(xn, L0_attn_Wq, L0_attn_bq, L0_attn_Wk, L0_attn_bk, L0_attn_Wv, L0_attn_bv, L0_attn_Wo, L0_attn_bo) + _L0_ffn_ref(xn, L0_ffn_Wm, L0_ffn_bm, L0_ffn_expert_emb, L0_ffn_W1, L0_ffn_b1, L0_ffn_W2, L0_ffn_b2, L0_ffn_Wo, L0_ffn_bo)
    return x

_drawn_inputs = setup_inputs


def setup_inputs(seed=0):
    import zlib

    import numpy as np

    out = dict(_drawn_inputs(seed))
    spreads = {'L0_ffn_bm': (0.0, 0.1),
     'L0_ffn_b1': (0.0, 0.1),
     'L0_ffn_b2': (0.0, 0.1),
     'L0_ffn_bo': (0.0, 0.1)}
    factors = {'L0_attn_bq': 38.231, 'L0_attn_bk': 64.0, 'L0_attn_bv': 5.843, 'L0_attn_bo': 6.164}
    for name, (base, spread) in spreads.items():
        noise = np.random.default_rng([zlib.crc32(name.encode()), seed]).standard_normal(out[name].shape)
        drawn = base * np.exp(spread * noise) if base else spread * noise
        out[name] = jnp.asarray(drawn.astype(out[name].dtype))
    for name, factor in factors.items():
        out[name] = (out[name] * factor).astype(out[name].dtype)
    return out
```

```python
from contextlib import ExitStack

import concourse.bass as bass
from concourse import mybir

F32 = mybir.dt.float32
BF16 = mybir.dt.bfloat16
U32 = mybir.dt.uint32
ALU = mybir.AluOpType
ACT = mybir.ActivationFunctionType
AX = mybir.AxisListType

B, N, D = 16, 512, 128
P = 128
NT = N // P
AH, AD = 16, 8
NG = AH // 2
BZ = 64
NBK = N // BZ
FH, FD = 8, 16
NE, HID = 16, 64
NTILE = NE * HID // P
EPS = 1e-5
SCALE = float(AD) ** -0.5
TERMS = [(0, 0), (0, 1), (0, 2), (1, 0), (1, 1), (2, 0)]
QK_ROWS = len(TERMS) * AD
HALF = 64
FFN_ROWS = len(TERMS) * FD
GATE_ROWS = 3 * NE
BIG = 3.0e38
HEAD_ORDER = [0, 2, 4, 6, 1, 3, 5, 7]
GROUPS = FH * NTILE // 2
G_RING = 8

UNITS = [[(0, 0), (1, 128), (7, 320), (2, 512), (3, 768)], [(4, 0), (5, 256), (6, 512)]]
UNIT_WIDTH = [1024, 768]
PAIR_WIDTH = sum(UNIT_WIDTH)


def query_runs(m):
    if m < 3:
        return [(0, BZ * (m + 2))]
    last = min(m + 1, NBK - 1)
    return [(0, BZ), (BZ * (m - 1), BZ * (last - m + 2))]


def key_range(i):
    if i == 0:
        return 0, N
    return BZ * (i - 1), BZ * min(i + 2, NBK)


CHUNKS = [[(0, 0)], [(1, 0), (2, 192), (7, 384)], [(3, 0), (4, 192)], [(5, 0), (6, 192)]]
REDUCES = [[(0, 0, 1, 512)], [(1, 0, 2, 192), (7, 384, 1, 128)], [(3, 0, 2, 192)], [(5, 0, 2, 192)]]
FIRST_CHUNK_GROUP = 11


C_PREP = 3
C_USES = 1 + C_PREP + 2
S_PREP = 3
S_USES = 1 + 4 * NG + 1 + S_PREP + 1


class Count:

    def __init__(self):
        self.base, self.n = 0, 0

    def up(self, k=1):
        self.n += k
        return self.base + self.n

    @property
    def now(self):
        return self.base + self.n


def over_batches(eng, counts, prologue, body):
    prologue()
    before = [c.n for c in counts]
    body(0, True)
    per = [c.n - k for c, k in zip(counts, before)]
    with eng.Fori(1, B - 1, 1) as b:
        for c, k, p in zip(counts, before, per):
            c.base, c.n = b * p + k, 0
        body(b, True)
    for c, k, p in zip(counts, before, per):
        c.base, c.n = (B - 1) * p + k, 0
    body(B - 1, False)


def wait(eng, sem, value):
    if not (isinstance(value, int) and value <= 0):
        eng.wait_ge(sem, value)


def program(nc, x, wq, bq, wk, bk, wv, bv, wo_a, wm, bm, emb, w1b1, w2, b2, wo_f, bo_a, bo_f,
            ident_d, gate_spread_d, head_sum_d, den_spread_d, rank_d, minus_d, zero_d, out):
    with ExitStack() as ctx:
        def sb(name, shape, dt=F32):
            return ctx.enter_context(nc.sbuf_tensor(name, shape, dt))

        def ps(name, shape):
            return ctx.enter_context(nc.psum_tensor(name, shape, F32))

        def sem(name):
            return ctx.enter_context(nc.semaphore(name))

        wq_sb, wk_sb, wv_sb, wm_sb, wof_sb = (sb(n, [P, D]) for n in ("wq", "wk", "wv", "wm", "wof"))
        woa_sb = sb("woa", [P, 2, D])
        bias3 = sb("bias3", [P, 3])
        bv_sb = sb("bv", [P, D])
        bo_two = sb("bo_two", [P, 2, D])
        bo_sb = sb("bo", [P, D])
        emb_sb = sb("emb", [P, P])
        arena = sb("arena", [P, 2 * G_RING * 2 * N])
        hid = arena[:, 0:G_RING * 2 * N].rearrange("p (r a n) -> p r a n", a=2, n=N)
        gated = arena[:, G_RING * 2 * N:].rearrange("p (h n) -> p h n", n=N)
        prob = arena[:, 0:NG * PAIR_WIDTH].rearrange("p (g w) -> p g w", g=NG)
        w1raw = arena[0:FD + 1, 0:NE * HID]
        w1tmp = arena[0:FD + 1, NE * HID:2 * NE * HID]
        w1parts = arena[0:FD + 1, 2 * NE * HID:4 * NE * HID].bitcast(BF16)[:, 0:3 * NE * HID].rearrange(
            "p (c n) -> p c n", c=3)
        w1_st = sb("w1_st", [FFN_ROWS + 3, NE * HID], BF16)
        w2_sb = sb("w2", [P, NTILE, 32])
        b2_sb = sb("b2", [P, P])
        ident = sb("ident", [P, P])
        gate_spread = sb("gate_spread", [P, 4, P], BF16)
        head_sum = sb("head_sum", [P, 2, 32])
        den_spread = sb("den_spread", [P, P])
        rank = sb("rank", [P, NT * FH * NE])
        minus_half = sb("minus_half", [P, NT])

        xt = sb("xt", [P, NT, D])
        idle = sb("idle", [P, 1])
        zero_col = sb("zero_col", [P, 1])
        stats = sb("stats", [P, NT, 6])
        mean_var = sb("mean_var", [P, NT, 2])
        var_eps = sb("var_eps", [P, NT])
        rstd = sb("rstd", [P, NT])
        xn = sb("xn", [P, NT, D])
        xnT = sb("xnT", [P, N])
        q32, k32, t32, gT32 = (sb(n, [P, N]) for n in ("q32", "k32", "t32", "gT32"))
        qk_tmp, dve_tmp = sb("qk_tmp", [P, N]), sb("dve_tmp", [P, N])
        q_parts, k_parts, t_parts, g_parts = (sb(n, [P, 3, N], BF16) for n in
                                              ("q_parts", "k_parts", "t_parts", "g_parts"))
        rt = [P, NT * FH * NE]
        z, pz, c1, one1, z2, one2 = (sb(n, rt) for n in ("z", "pz", "c1", "one1", "z2", "one2"))
        top = sb("top", [P, 8, NT * FH])

        t_st = sb("t_st", [FFN_ROWS + 3, FH, N], BF16)
        g_st = sb("g_st", [P, FH // 2, N], BF16)
        q_st = sb("q_st", [P, NG, N], BF16)
        k_dg = sb("k_dg", [P, 2, NG, N], BF16)
        v_dg = sb("v_dg", [P, NBK, NG, 32])

        gates = sb("gates", [P, 2, N])
        mx = sb("mx", [P, P])
        mT32, m_tmp = sb("mT32", [NG * NBK, P]), sb("m_tmp", [NG * NBK, P])
        m_parts = sb("m_parts", [NG * NBK, 3, P], BF16)
        combT = sb("combT", [P, N])
        o_sb = sb("o_sb", [P, 2, N])
        rden = sb("rden", [P, 2, N])
        o_nrm = sb("o_nrm", [P, 2, N])
        xr = sb("xr", [P, NT, D])
        xb = sb("xb", [P, NT, D])
        y = sb("y", [P, NT, D])

        ring = ps("ring", [P, 2, 2, N])
        u_bank, g_bank, s_bank, c_bank = (ps(n, [P, N]) for n in ("u_bank", "g_bank", "s_bank", "c_bank"))

        const_in = sem("const_in")
        made = sem("made")
        w1_split = sem("w1_split")
        w1_in = sem("w1_in")
        x_in, xr_in = sem("x_in"), sem("xr_in")
        var_ready, rstd_ready, xn_ready = sem("var_ready"), sem("rstd_ready"), sem("xn_ready")
        q_split, k_split = sem("q_split"), sem("k_split")
        t_split, g_split, m_split = sem("t_split"), sem("g_split"), sem("m_split")
        t_in, g_in, qk_in, m_in = sem("t_in"), sem("g_in"), sem("qk_in"), sem("m_in")
        pz_ready = sem("pz_ready")
        gate_ready = sem("gate_ready")
        v_ready = sem("v_ready")
        ring_full, ring_free = sem("ring_full"), sem("ring_free")
        u_full, u_free = sem("u_full"), sem("u_free")
        g_full, g_free = sem("g_full"), sem("g_free")
        s_full, s_free = sem("s_full"), sem("s_free")
        c_full, c_free = sem("c_full"), sem("c_free")
        hid_ready, gated_ready, prob_ready = sem("hid_ready"), sem("gated_ready"), sem("prob_ready")
        comb_ready, o_ready, on_ready = sem("comb_ready"), sem("o_ready"), sem("on_ready")
        xb_ready, y_out = sem("xb_ready"), sem("y_out")
        dve_done, act_done, pool_done = sem("dve_done"), sem("act_done"), sem("pool_done")

        x_rows = x.rearrange("(b t p) d -> b p t d", p=P, t=NT)
        out_rows = out.rearrange("(b t p) d -> b p t d", p=P, t=NT)

        loads = [
            (wm_sb[:, :], wm), (ident[:, :], ident_d), (wq_sb[:, :], wq), (wk_sb[:, :], wk),
            (bias3[:, 0:1], bq), (bias3[:, 1:2], bk), (bias3[:, 2:3], bm), (emb_sb[:, :], emb),
            (w1raw[:, :], w1b1), (rank[:, :], rank_d.broadcast_to([P, NT * FH * NE])),
            (wv_sb[:, :], wv), (bv_sb[:, :], bv.broadcast_to([P, D])),
            (w2_sb[:, :, :], w2), (b2_sb[:, :], b2), (gate_spread[:, :, :], gate_spread_d),
            (head_sum[:, :, :], head_sum_d), (den_spread[:, :], den_spread_d),
            (wof_sb[:, :], wo_f), (woa_sb[:, :, :], wo_a),
            (bo_two[:, 0, :], bo_a.broadcast_to([P, D])), (bo_two[:, 1, :], bo_f.broadcast_to([P, D])),
        ]
        N_MADE = 7

        block = ctx.enter_context(nc.Block())

        @block.sync
        def _(sp):
            x_used, xr_used, y_seen = Count(), Count(), Count()
            q_s, k_s, t_s, g_s, m_s = Count(), Count(), Count(), Count(), Count()
            ring_seen = Count()
            counts = [x_used, xr_used, y_seen, q_s, k_s, t_s, g_s, m_s, ring_seen]

            def load_x(b):
                wait(sp, xn_ready, x_used.now)
                x_used.up()
                sp.dma_start(xt[:, :, :], x_rows[b]).then_inc(x_in, 16)

            def restack_ffn():
                sp.wait_ge(t_split, t_s.up())
                for s, (part, _) in enumerate(TERMS):
                    sp.dma_start(t_st[FD * s:FD * (s + 1), :, :], t_parts[:, part, :]).then_inc(t_in, 16)
                sp.wait_ge(g_split, g_s.up())
                for ab in range(2):
                    for part in range(3):
                        r = HALF * ab + NE * part
                        sp.dma_start(g_st[r:r + NE, :, :],
                                     g_parts[HALF * ab:HALF * (ab + 1), part, :]).then_inc(g_in, 16)

            def restack_qk():
                wait(sp, ring_full, ring_seen.now)
                for ab in range(2):
                    r = HALF * ab + QK_ROWS
                    sp.dma_start(q_st[r:r + 3, :, :], zero_d).then_inc(qk_in, 16)
                sp.wait_ge(q_split, q_s.up())
                for ab in range(2):
                    for s, (part, _) in enumerate(TERMS):
                        r = HALF * ab + AD * s
                        sp.dma_start(q_st[r:r + AD, :, :],
                                     q_parts[HALF * ab:HALF * (ab + 1), part, :]).then_inc(qk_in, 16)
                sp.wait_ge(k_split, k_s.up())
                for ab in range(2):
                    for s, (_, part) in enumerate(TERMS):
                        r = HALF * ab + AD * s
                        sp.dma_start(k_dg[r:r + AD, ab, :, :],
                                     k_parts[HALF * ab:HALF * (ab + 1), part, :]).then_inc(qk_in, 16)

            def prologue():
                y_seen.up(S_PREP)
                load_x(0)
                for dst, src in loads:
                    sp.dma_start(dst, src).then_inc(const_in, 16)
                sp.wait_ge(made, N_MADE)
                for ab in range(2):
                    r = HALF * ab + QK_ROWS
                    sp.dma_start(k_dg[r:r + 3, ab, :, :], minus_d).then_inc(w1_in, 16)
                sp.wait_ge(w1_split, 1)
                for s, (_, part) in enumerate(TERMS):
                    sp.dma_start(w1_st[FD * s:FD * (s + 1), :], w1parts[0:FD, part, :]).then_inc(w1_in, 16)
                for part in range(3):
                    r = FFN_ROWS + part
                    sp.dma_start(w1_st[r:r + 1, :], w1parts[FD:FD + 1, part, :]).then_inc(w1_in, 16)
                restack_ffn()

            def body(b, more):
                restack_qk()
                wait(sp, xb_ready, xr_used.now)
                xr_used.up()
                sp.dma_start(xr[:, :, :], x_rows[b]).then_inc(xr_in, 16)
                if more:
                    load_x(b + 1)
                sp.wait_ge(m_split, m_s.up())
                for ab in range(2):
                    for part in range(3):
                        r = HALF * ab + QK_ROWS + part
                        sp.dma_start(q_st[r:r + 1, :, :],
                                     m_parts[:, part, HALF * ab:HALF * (ab + 1)]).then_inc(m_in, 16)
                ring_seen.up(GROUPS + 2 * NG)
                if more:
                    restack_ffn()
                sp.wait_ge(s_free, y_seen.up(S_USES if more else S_USES - S_PREP))
                sp.dma_start(out_rows[b], y[:, :, :]).then_inc(y_out, 16)

            over_batches(sp, counts, prologue, body)
            sp.wait_ge(y_out, 16 * B)

        @block.gpsimd
        def _(pool):
            step = Count()
            var_s, q_s, k_s, xr_s, q_in_s, s_s, c_s = (Count() for _ in range(7))
            counts = [step, var_s, q_s, k_s, xr_s, q_in_s, s_s, c_s]

            def link(ins):
                ins.then_inc(pool_done, 1)
                pool.wait_ge(pool_done, step.up())

            def power():
                pool.wait_ge(var_ready, var_s.up())
                nc.gpsimd.tensor_tensor(rstd[:, :], var_eps[:, :], minus_half[:, :], ALU.pow).then_inc(rstd_ready, 1)

            zeros = zero_col[:, :].broadcast_to([P, N])

            def split(src, parts, done):
                link(nc.gpsimd.tensor_tensor(parts[:, 0, :], src, zeros, ALU.add))
                link(nc.gpsimd.tensor_tensor(qk_tmp[:, :], src, parts[:, 0, :], ALU.subtract))
                link(nc.gpsimd.tensor_tensor(parts[:, 1, :], qk_tmp[:, :], zeros, ALU.add))
                nc.gpsimd.tensor_tensor(parts[:, 2, :], qk_tmp[:, :], parts[:, 1, :], ALU.subtract).then_inc(done, 1)

            def split_qk(q_use, k_use):
                wait(pool, qk_in, q_in_s.now)
                q_in_s.up(26 * 16)
                pool.wait_ge(s_free, s_s.up(q_use))
                split(q32[:, :], q_parts, q_split)
                pool.wait_ge(q_split, q_s.up())
                pool.wait_ge(c_free, c_s.up(k_use))
                split(k32[:, :], k_parts, k_split)
                pool.wait_ge(k_split, k_s.up())

            def prologue():
                nc.gpsimd.memset(zero_col[:, :], 0.0).then_inc(made, 1)
                nc.gpsimd.memset(minus_half[:, :], -0.5).then_inc(made, 1)
                nc.gpsimd.memset(q_st[:, :, :].bitcast(U32), 0).then_inc(made, 1)
                nc.gpsimd.memset(k_dg[:, :, :, :].bitcast(U32), 0).then_inc(made, 1)
                pool.wait_ge(const_in, 16 * len(loads))
                pool.wait_ge(made, N_MADE)
                nc.gpsimd.tensor_tensor(bo_sb[:, :], bo_two[:, 0, :], bo_two[:, 1, :], ALU.add).then_inc(made, 1)
                pool.wait_ge(made, N_MADE + 1)
                power()
                split_qk(S_PREP, C_PREP)

            def body(b, more):
                pool.wait_ge(xr_in, xr_s.up(16))
                wait(pool, s_free, s_s.now)
                for j in range(NT):
                    ins = nc.gpsimd.tensor_tensor(xb[:, j, :], xr[:, j, :], bo_sb[:, :], ALU.add)
                ins.then_inc(xb_ready, 1)
                if more:
                    power()
                    split_qk(S_USES - 1, C_USES - 2)
                    s_s.up()
                    c_s.up(2)

            over_batches(pool, counts, prologue, body)

        @block.scalar
        def _(act):
            ring_s, l2_s, z_s, xnT_s, used = Count(), Count(), Count(), Count(), Count()
            counts = [ring_s, l2_s, z_s, xnT_s, used]

            def gate_exp(use=S_PREP - 1, later=1):
                act.wait_ge(s_free, z_s.up(use))
                z_s.up(later)
                nc.scalar.activation(pz[:, :], z[:, :], ACT.Exp).then_inc(pz_ready, 1)

            def body(b, more):
                for gi in range(GROUPS):
                    act.wait_ge(ring_full, ring_s.up())
                    if gi % 2 == 0:
                        wait(act, u_full, l2_s.now + (gi - G_RING) // 2 + 1 if gi >= G_RING else l2_s.now)
                    nc.scalar.activation(hid[:, gi % G_RING, :, :], ring[:, gi % 2, :, :], ACT.Gelu).then_inc(hid_ready, 1)
                    used.up()
                l2_s.up(2 * FH + 1)
                for g in range(NG):
                    for n in range(2):
                        act.wait_ge(ring_full, ring_s.up())
                        at = n * UNIT_WIDTH[0]
                        src = ring[:, n, :, :].rearrange("p a n -> p (a n)")[:, 0:UNIT_WIDTH[n]]
                        nc.scalar.activation(prob[:, g, at:at + UNIT_WIDTH[n]], src, ACT.Exp).then_inc(prob_ready, 1)
                    if more and g == 3:
                        gate_exp(S_USES - 2, 2)

            over_batches(act, counts, gate_exp, body)

        @block.vector
        def _(dve):
            step = Count()
            x_s, r_s, sf, cf, uf, gf, pz_s = (Count() for _ in range(7))
            m_s, t_s, g_s, t_in_s, g_in_s, m_in_s, xb_s, y_s, comb_s, v_s, o_s = (Count() for _ in range(11))
            counts = [step, x_s, r_s, sf, cf, uf, gf, pz_s, m_s, t_s, g_s, t_in_s, g_in_s, m_in_s, xb_s, y_s,
                      comb_s, v_s, o_s]

            def link(ins):
                ins.then_inc(dve_done, 1)
                dve.wait_ge(dve_done, step.up())

            def split(src, parts, tmp, done):
                link(nc.vector.tensor_copy(parts[:, 0, :], src))
                link(nc.vector.tensor_tensor(tmp, src, parts[:, 0, :], ALU.subtract))
                link(nc.vector.tensor_copy(parts[:, 1, :], tmp))
                nc.vector.tensor_tensor(parts[:, 2, :], tmp, parts[:, 1, :], ALU.subtract).then_inc(done, 1)

            def norm_stats():
                dve.wait_ge(x_in, x_s.up(16))
                for j in range(NT):
                    ins = nc.vector.bn_stats(stats[:, j, :], xt[:, j, :])
                link(ins)
                nc.vector.tensor_copy(idle[:, :], bias3[:, 0:1])
                for j in range(NT):
                    ins = nc.vector.bn_aggr(mean_var[:, j, :], stats[:, j, :])
                link(ins)
                nc.vector.tensor_scalar(var_eps[:, :], mean_var[:, :, 1], EPS, None, ALU.add).then_inc(var_ready, 1)

            def normalise():
                dve.wait_ge(rstd_ready, r_s.up())
                for j in range(NT):
                    ins = nc.vector.tensor_scalar(xn[:, j, :], xt[:, j, :], mean_var[:, j, 0:1], rstd[:, j:j + 1],
                                                  ALU.subtract, ALU.mult)
                ins.then_inc(xn_ready, 1)

            def take_xnT():
                dve.wait_ge(s_full, sf.up())
                nc.vector.tensor_copy(xnT[:, :], s_bank[:, :]).then_inc(s_free, 1)

            def take_t():
                dve.wait_ge(c_full, cf.up())
                nc.vector.tensor_scalar(t32[:, :], c_bank[:, :], bias3[:, 2:3], None, ALU.add).then_inc(c_free, 1)
                dve.wait_ge(c_free, cf.now)
                wait(dve, t_in, t_in_s.now)
                t_in_s.up(16 * len(TERMS))
                split(t32[:, :], t_parts, dve_tmp[:, :], t_split)
                dve.wait_ge(t_split, t_s.up())

            def take_q():
                dve.wait_ge(s_full, sf.up())
                nc.vector.tensor_scalar(q32[:, :], s_bank[:, :], bias3[:, 0:1], SCALE, ALU.add, ALU.mult).then_inc(s_free, 1)

            def take_k():
                dve.wait_ge(c_full, cf.up())
                nc.vector.tensor_scalar(k32[:, :], c_bank[:, :], bias3[:, 1:2], None, ALU.add).then_inc(c_free, 1)

            R = NT * FH // 4

            def by_expert(t):
                return t[:, :].rearrange("p (r e h) -> p r h e", r=R, h=4)

            def per_head(k, spread=True):
                v = top[:, k, :].rearrange("p (r h) -> p r h", h=4)
                return v.unsqueeze(3).broadcast_to([P, R, 4, NE]) if spread else v

            def route():
                dve.wait_ge(s_full, sf.up())
                zp = s_bank[:, :].rearrange("p (r e h) -> p r h e", r=R, h=4)
                link(nc.vector.tensor_reduce(per_head(0, False), zp, AX.X, ALU.max))
                nc.vector.tensor_tensor(by_expert(z), zp, per_head(0), ALU.subtract).then_inc(s_free, 1)
                dve.wait_ge(s_free, sf.now)
                for n, (zz, one) in enumerate([(z, one1), (z2, one2)]):
                    if n == 0:
                        link(nc.vector.scalar_tensor_tensor(c1[:, :], z[:, :], 0.0, rank[:, :], ALU.is_equal, ALU.mult))
                    else:
                        link(nc.vector.scalar_tensor_tensor(z2[:, :], one1[:, :], -BIG, z[:, :], ALU.mult, ALU.add))
                        link(nc.vector.tensor_reduce(per_head(1, False), by_expert(z2), AX.X, ALU.max))
                        link(nc.vector.tensor_tensor(by_expert(one2), by_expert(z2), per_head(1), ALU.is_equal))
                        link(nc.vector.tensor_tensor(c1[:, :], one2[:, :], rank[:, :], ALU.mult))
                    link(nc.vector.tensor_reduce(per_head(2 + n, False), by_expert(c1), AX.X, ALU.max))
                    link(nc.vector.tensor_tensor(by_expert(one), by_expert(c1), per_head(2 + n), ALU.is_equal))
                link(nc.vector.tensor_tensor(c1[:, :], one1[:, :], one2[:, :], ALU.add))
                dve.wait_ge(pz_ready, pz_s.up())
                link(nc.vector.tensor_reduce(per_head(4, False), by_expert(pz), AX.X, ALU.add))
                link(nc.vector.reciprocal(top[:, 5, :], top[:, 4, :]))
                link(nc.vector.tensor_tensor(z2[:, :], pz[:, :], c1[:, :], ALU.mult))
                nc.vector.tensor_tensor(by_expert(c1), by_expert(z2), per_head(5), ALU.mult).then_inc(gate_ready, 1)

            def take_gates():
                dve.wait_ge(c_full, cf.up())
                nc.vector.tensor_copy(gT32[:, :], c_bank[:, :]).then_inc(c_free, 1)
                dve.wait_ge(c_free, cf.now)
                wait(dve, g_in, g_in_s.now)
                g_in_s.up(16 * 6)
                split(gT32[:, :], g_parts, dve_tmp[:, :], g_split)
                dve.wait_ge(g_split, g_s.up())

            def take_v():
                dve.wait_ge(s_full, sf.up())
                for m in range(NBK):
                    for ab in range(2):
                        rows = slice(HALF * ab, HALF * (ab + 1))
                        src = s_bank[rows, m * HALF:(m + 1) * HALF].rearrange("p (g d) -> p g d", d=AD)
                        bias = bv_sb[rows, HALF * ab:HALF * (ab + 1)].rearrange("p (g d) -> p g d", d=AD)
                        ins = nc.vector.tensor_tensor(v_dg[rows, m, :, 16 * ab:16 * ab + AD], src, bias, ALU.add)
                ins.then_inc(s_free, 1)

            def take_max(g, c):
                dve.wait_ge(s_full, sf.up())
                for i, col, n, width in REDUCES[c]:
                    at = g * NBK + i
                    ins = nc.vector.tensor_reduce(mx[:, at:at + n],
                                                  s_bank[:, col:col + n * width].rearrange("p (n w) -> p n w", n=n),
                                                  AX.X, ALU.max)
                ins.then_inc(s_free, 1)

            def take_mT():
                rows = slice(0, NG * NBK)
                dve.wait_ge(s_full, sf.up())
                nc.vector.tensor_copy(mT32[:, :], s_bank[rows, 0:P]).then_inc(s_free, 1)
                dve.wait_ge(s_free, sf.now)
                wait(dve, m_in, m_in_s.now)
                m_in_s.up(16 * 6)
                split(mT32[:, :], m_parts, m_tmp[:, :], m_split)
                dve.wait_ge(m_split, m_s.up())

            def gate_half(n):
                dve.wait_ge(g_full, gf.up())
                nc.vector.tensor_copy(gates[:, n % 2, :], g_bank[:, :]).then_inc(g_free, 1)
                dve.wait_ge(g_free, gf.now)
                dve.wait_ge(u_full, uf.up())
                nc.vector.tensor_tensor(gated[:, n, :], u_bank[:, :], gates[:, n % 2, :], ALU.mult).then_inc(u_free, 1)

            def take_comb():
                dve.wait_ge(c_full, cf.up())
                nc.vector.tensor_copy(combT[:, :], c_bank[:, :]).then_inc(c_free, 1)

            def take_o(grp):
                bank, full, free, cnt = ((u_bank, u_full, u_free, uf), (g_bank, g_full, g_free, gf))[grp]
                dve.wait_ge(full, cnt.up())
                nc.vector.tensor_copy(o_sb[:, grp, :], bank[:, :]).then_inc(free, 1)

            def normalise_o(grp):
                dve.wait_ge(c_full, cf.up())
                nc.vector.reciprocal(rden[:, grp, :], c_bank[:, :]).then_inc(c_free, 1)
                dve.wait_ge(c_free, cf.now)
                nc.vector.tensor_tensor(o_nrm[:, grp, :], o_sb[:, grp, :], rden[:, grp, :], ALU.mult).then_inc(on_ready, 1)

            def finish():
                dve.wait_ge(xb_ready, xb_s.up())
                wait(dve, y_out, y_s.now)
                y_s.up(16)
                dve.wait_ge(s_full, sf.up())
                ins = nc.vector.tensor_tensor(y[:, :, :].rearrange("p t d -> p (t d)"), s_bank[:, :],
                                              xb[:, :, :].rearrange("p t d -> p (t d)"), ALU.add)
                ins.then_inc(s_free, 1)

            def prologue():
                nc.vector.memset(t_st[:, :, :], 1.0).then_inc(made, 1)
                nc.vector.memset(g_st[:, :, :].bitcast(U32), 0).then_inc(made, 1)
                nc.vector.memset(v_dg[:, :, :, :], 0.0).then_inc(made, 1)
                nc.vector.memset(mx[:, :], 0.0)
                dve.wait_ge(made, N_MADE)
                for ab in range(2):
                    rows = slice(HALF * ab, HALF * (ab + 1))
                    ins = nc.vector.memset(v_dg[rows, :, :, 16 * ab + AD:16 * ab + AD + 1], 1.0)
                link(ins)
                dve.wait_ge(const_in, 16 * len(loads))
                norm_stats()
                split(w1raw[:, :], w1parts, w1tmp[:, :], w1_split)
                normalise()
                take_xnT()
                take_t()
                route()
                take_q()
                take_gates()
                take_k()

            def body(b, more):
                half = 0
                chunk = 0
                take_v()
                for gi in range(GROUPS + 3):
                    while chunk < 4 * NG and gi < GROUPS and FIRST_CHUNK_GROUP + chunk // 2 <= gi:
                        take_max(chunk // 4, chunk % 4)
                        chunk += 1
                    if gi >= 3 and gi % 2 == 1 or gi == GROUPS + 2:
                        pass
                    if gi % 2 == 1 and gi >= 3:
                        gate_half(half)
                        half += 1
                    if gi == FIRST_CHUNK_GROUP + 2 * NG:
                        take_mT()
                assert half == 2 * FH
                take_comb()
                if more:
                    norm_stats()
                    normalise()
                    take_xnT()
                    take_t()
                    route()
                    take_q()
                    take_gates()
                    take_k()
                take_o(0)
                normalise_o(0)
                take_o(1)
                normalise_o(1)
                finish()

            over_batches(dve, counts, prologue, body)

        @block.tensor
        def _(pe):
            mm = nc.tensor.matmul
            xn_s, s_uses, c_uses, u_uses, g_uses, ring_uses = (Count() for _ in range(6))
            gate_s, hid_s, prob_s, gated_s, t_in_s, g_in_s, qk_s, m_s, o_s, on_s, y_s = (Count() for _ in range(11))
            counts = [xn_s, s_uses, c_uses, u_uses, g_uses, ring_uses, gate_s, hid_s, prob_s, gated_s, t_in_s, g_in_s,
                      qk_s, m_s, o_s, on_s, y_s]

            def claim(free, uses):
                wait(pe, free, uses.now)
                uses.up()

            def turn_xn():
                pe.wait_ge(xn_ready, xn_s.up())
                claim(s_free, s_uses)
                for j in range(NT):
                    ins = nc.tensor.transpose(s_bank[:, j * P:(j + 1) * P], xn[:, j, :], ident[:, :])
                ins.then_inc(s_full, 1)

            def project(weight, bank, free, uses, full):
                claim(free, uses)
                mm(bank[:, :], weight[:, :], xnT[:, :], start=True, stop=True).then_inc(full, 1)

            def project_t():
                wait(pe, s_free, s_uses.now)
                project(wm_sb, c_bank, c_free, c_uses, c_full)

            def logits():
                wait(pe, c_free, c_uses.now)
                claim(s_free, s_uses)
                for j in range(NT):
                    ins = mm(s_bank[:, j * P:(j + 1) * P], t32[:, j * P:(j + 1) * P], emb_sb[:, :], start=True, stop=True)
                ins.then_inc(s_full, 1)

            def turn_gates():
                pe.wait_ge(gate_ready, gate_s.up())
                claim(c_free, c_uses)
                for j in range(NT):
                    ins = nc.tensor.transpose(c_bank[:, j * P:(j + 1) * P], c1[:, j * P:(j + 1) * P], ident[:, :])
                ins.then_inc(c_full, 1)

            def values():
                claim(s_free, s_uses)
                for m in range(NBK):
                    for ab in range(2):
                        ins = mm(s_bank[HALF * ab:HALF * (ab + 1), m * HALF:(m + 1) * HALF],
                                 xnT[:, m * BZ:(m + 1) * BZ], wv_sb[:, HALF * ab:HALF * (ab + 1)], start=True, stop=True)
                ins.then_inc(s_full, 1)

            def score_chunk(g, c):
                claim(s_free, s_uses)
                for i, col in CHUNKS[c]:
                    lo, hi = key_range(i)
                    for ab in range(2):
                        ins = mm(s_bank[HALF * ab:HALF * (ab + 1), col:col + hi - lo],
                                 q_st[:, g, i * BZ:(i + 1) * BZ], k_dg[:, ab, g, lo:hi], start=True, stop=True)
                ins.then_inc(s_full, 1)

            def turn_max():
                claim(s_free, s_uses)
                nc.tensor.transpose(s_bank[:, 0:P], mx[:, :], ident[:, :]).then_inc(s_full, 1)

            def hidden(gi):
                claim(ring_free, ring_uses) if False else None
                h = HEAD_ORDER[gi // 4]
                for a in range(2):
                    t = 2 * (gi % 4) + a
                    ins = mm(ring[:, gi % 2, a, :], w1_st[:, t * P:(t + 1) * P], t_st[:, h, :], start=True, stop=True)
                ins.then_inc(ring_full, 1)

            def second(n):
                h, u = HEAD_ORDER[n // 2], n % 2
                claim(g_free, g_uses)
                mm(g_bank[:, :], gate_spread[0:HALF + GATE_ROWS, 2 * (h % 2) + u, :], g_st[0:HALF + GATE_ROWS, h // 2, :],
                   start=True, stop=True).then_inc(g_full, 1)
                claim(u_free, u_uses)
                pe.wait_ge(hid_ready, hid_s.now + 2 * (n + 1))
                for a in range(4):
                    t = 4 * u + a
                    slot = (2 * n + a // 2) % G_RING
                    ins = mm(u_bank[32 * a:32 * (a + 1), :], w2_sb[:, t, :], hid[:, slot, a % 2, :], start=True, stop=True)
                ins.then_inc(u_full, 1)

            def combine(group):
                pe.wait_ge(u_free, u_uses.now)
                for u in range(2):
                    for q in range(4):
                        ins = mm(c_bank[32 * q:32 * (q + 1), :], head_sum[:, group, :], gated[:, 8 * group + 2 * q + u, :],
                                 start=False, stop=(group == 1 and u == 1), skip_group_check=True)
                return ins

            def shifted(g, n):
                wait(pe, prob_ready if g or n else ring_free, 0)
                for m, col in UNITS[n]:
                    for lo, width in query_runs(m):
                        bank, c0 = col // N, col % N
                        for ab in range(2):
                            ins = mm(ring[HALF * ab:HALF * (ab + 1), n, bank, c0:c0 + width],
                                     k_dg[:, ab, g, m * BZ:(m + 1) * BZ], q_st[:, g, lo:lo + width],
                                     start=True, stop=True)
                        col += width
                ins.then_inc(ring_full, 1)

            def attend(grp, ms, first, last):
                bank = (u_bank, g_bank)[grp]
                for m in ms:
                    for lo, width in query_runs(m):
                        n = next(k for k in range(2) if m in [a for a, _ in UNITS[k]])
                        col = dict(UNITS[n])[m] + n * UNIT_WIDTH[0]
                        off = 0 if lo == 0 else BZ
                        for q in range(4):
                            ins = mm(bank[32 * q:32 * (q + 1), lo:lo + width], v_dg[:, m, 4 * grp + q, :],
                                     prob[:, 4 * grp + q, col + off:col + off + width],
                                     start=(m == 0), stop=(m == NBK - 1), skip_group_check=True)
                if last:
                    ins.then_inc((u_full, g_full)[grp], 1)

            def spread_den(grp):
                wait(pe, (u_free, g_free)[grp], (u_uses, g_uses)[grp].now)
                claim(c_free, c_uses)
                mm(c_bank[:, :], den_spread[:, :], o_sb[:, grp, :], start=True, stop=True).then_inc(c_full, 1)

            def project_out():
                claim(s_free, s_uses)
                pe.wait_ge(on_ready, on_s.up(2))
                for j in range(NT):
                    tok = slice(j * P, (j + 1) * P)
                    mm(s_bank[:, tok], combT[:, tok], wof_sb[:, :], start=True, stop=False)
                    for grp in range(2):
                        ins = mm(s_bank[:, tok], o_nrm[:, grp, tok], woa_sb[:, grp, :], start=False, stop=(grp == 1))
                ins.then_inc(s_full, 1)

            def prologue():
                pe.wait_ge(const_in, 16 * len(loads))
                pe.wait_ge(made, N_MADE)
                turn_xn()
                project_t()
                logits()
                project(wq_sb, s_bank, s_free, s_uses, s_full)
                turn_gates()
                project(wk_sb, c_bank, c_free, c_uses, c_full)
                pe.wait_ge(w1_in, 16 * 11)

            def body(b, more):
                values()
                pe.wait_ge(t_in, t_in_s.up(16 * len(TERMS)))
                claim(c_free, c_uses)
                mm(c_bank[:, :], b2_sb[:, :], gT32[:, :], start=True, stop=False, skip_group_check=True)
                half, chunk = 0, 0
                for gi in range(GROUPS + 3):
                    if gi < GROUPS:
                        if gi < 2:
                            wait(pe, prob_ready, prob_s.now)
                        else:
                            pe.wait_ge(hid_ready, hid_s.now + gi - 1)
                        hidden(gi)
                    if gi == 2:
                        pe.wait_ge(g_in, g_in_s.up(16 * 6))
                    if gi == FIRST_CHUNK_GROUP:
                        pe.wait_ge(qk_in, qk_s.up(16 * 26))
                    while chunk < 4 * NG and gi < GROUPS and FIRST_CHUNK_GROUP + chunk // 2 <= gi:
                        score_chunk(chunk // 4, chunk % 4)
                        chunk += 1
                        if chunk % 2 == 1:
                            break
                    if gi % 2 == 1 and gi >= 3:
                        second(half)
                        half += 1
                    while chunk < 4 * NG and gi < GROUPS and FIRST_CHUNK_GROUP + chunk // 2 <= gi:
                        score_chunk(chunk // 4, chunk % 4)
                        chunk += 1
                    if gi == FIRST_CHUNK_GROUP + 2 * NG:
                        turn_max()
                    if gi == 21:
                        pe.wait_ge(u_free, u_uses.now)
                        combine(0)
                hid_s.up(GROUPS)
                combine(1).then_inc(c_full, 1)
                pe.wait_ge(m_in, m_s.up(16 * 6))
                for g in range(NG):
                    for n in range(2):
                        if g == 0:
                            pe.wait_ge(hid_ready, hid_s.now + n - 1)
                        else:
                            pe.wait_ge(prob_ready, prob_s.now + 2 * g + n - 1)
                        shifted(g, n)
                    if more:
                        if g == 0:
                            turn_xn()
                        if g == 1:
                            project_t()
                        if g == 2:
                            logits()
                        if g == 3:
                            project(wq_sb, s_bank, s_free, s_uses, s_full)
                        if g == 6:
                            turn_gates()
                        if g == 7:
                            project(wk_sb, c_bank, c_free, c_uses, c_full)
                    if g >= 4:
                        if g == 4:
                            pe.wait_ge(prob_ready, prob_s.now + 8)
                            claim(u_free, u_uses)
                        attend(0, [2 * (g - 4), 2 * (g - 4) + 1], g == 4, g == 7)
                claim(g_free, g_uses)
                pe.wait_ge(prob_ready, prob_s.up(2 * NG))
                attend(1, range(NBK), True, True)
                spread_den(0)
                spread_den(1)
                project_out()

            over_batches(pe, counts, prologue, body)


def kernel(**inputs):
    import ml_dtypes as _ml
    import numpy as _np
    import concourse.bacc as _bacc
    from concourse import mybir as _mybir
    from concourse.bass_utils import run_bass_kernel_spmd as _run

    a = {k: _np.asarray(v) for k, v in inputs.items()}
    f32 = _np.float32

    def pair_cols(w):
        return w.reshape(-1, NG, 2, AD).transpose(0, 2, 3, 1).reshape(-1, D)

    wv = a["L0_attn_Wv"].reshape(D, NG, 2, AD).transpose(0, 2, 1, 3).reshape(D, D)
    bv = a["L0_attn_bv"].reshape(NG, 2, AD).transpose(1, 0, 2).reshape(1, D)
    wo_a = _np.zeros((4, 2, 16, 2, D), f32)
    wo_a[:, :, :AD] = a["L0_attn_Wo"].reshape(2, 4, 2, AD, D).transpose(1, 2, 3, 0, 4)
    wm = a["L0_ffn_Wm"].reshape(D, FH, FD).transpose(0, 2, 1).reshape(D, D)
    bm = a["L0_ffn_bm"].reshape(FH, FD).T.reshape(D, 1)
    emb = _np.zeros((FD, FH // 2, 2, 2, NE, FH // 2), f32)
    b2 = _np.zeros((2, NE, FH // 2, FH // 2, 2, FD), f32)
    for hp in range(FH // 2):
        for ab in range(2):
            emb[:, hp, ab, ab, :, hp] = a["L0_ffn_expert_emb"]
            b2[ab, :, hp, hp, ab, :] = a["L0_ffn_b2"]
    w1b1 = _np.concatenate([a["L0_ffn_W1"].transpose(1, 0, 2).reshape(FD, NE * HID),
                            a["L0_ffn_b1"].reshape(1, NE * HID)])
    w2 = _np.zeros((2, HID, NTILE, 2, FD), f32)
    for k in range(2):
        w2[k, :, :, k, :] = a["L0_ffn_W2"].reshape(NTILE, 2, HID, FD)[:, k].transpose(1, 0, 2)
    gate_spread = _np.zeros((2, HALF, 2, 2, NE // 2, FD), _ml.bfloat16)
    for ab in range(2):
        for part in range(3):
            for e in range(NE):
                gate_spread[ab, NE * part + e, ab, e // 8, e % 8, :] = 1
    head_sum = _np.zeros((NE // 2, FD, 2, 2, FD), f32)
    for o in range(FD):
        for ab in range(2):
            head_sum[:, o, ab, ab, o] = 1
    den_spread = _np.zeros((8, 16, 8, 16), f32)
    for k in range(8):
        den_spread[k, AD, k, :] = 1
    arrays = {
        "x": a["L0_attn_x"].reshape(B * N, D),
        "wq": pair_cols(a["L0_attn_Wq"]), "bq": pair_cols(a["L0_attn_bq"]).reshape(D, 1),
        "wk": pair_cols(a["L0_attn_Wk"]), "bk": pair_cols(a["L0_attn_bk"]).reshape(D, 1),
        "wv": wv, "bv": bv, "wo_a": wo_a.reshape(P, 2, D), "wm": wm, "bm": bm,
        "emb": emb.reshape(P, P), "w1b1": w1b1, "w2": w2.reshape(P, NTILE, 32), "b2": b2.reshape(P, P),
        "wo_f": a["L0_ffn_Wo"], "bo_a": a["L0_attn_bo"].reshape(1, D), "bo_f": a["L0_ffn_bo"].reshape(1, D),
        "ident": _np.eye(P, dtype=f32), "gate_spread": gate_spread.reshape(P, 4, P),
        "head_sum": head_sum.reshape(P, 2, 32), "den_spread": den_spread.reshape(P, P),
        "rank": _np.tile(_np.repeat(_np.arange(NE, 0, -1, dtype=f32), FH // 2), 2 * NT).reshape(1, NT * FH * NE),
        "minus": _np.full((3, NG * N), -1, _ml.bfloat16),
        "zero": _np.zeros((3, NG * N), _ml.bfloat16),
    }
    nc = _bacc.Bacc("TRN2", target_bir_lowering=False, num_devices=1)
    feed, args = {}, []
    for name, v in arrays.items():
        v = _np.ascontiguousarray(v)
        feed[f"in_{name}"] = v
        args.append(nc.dram_tensor(f"in_{name}", v.shape, _mybir.dt.from_np(v.dtype), kind="ExternalInput").ap())
    args.append(nc.dram_tensor("out_0", (B * N, D), _mybir.dt.from_np(_np.dtype("float32")), kind="ExternalOutput").ap())
    program(nc, *args)
    r = _run(nc, [feed], core_ids=[0])
    return r.results[0]["out_0"].reshape(B, N, D)
```

```python
from contextlib import ExitStack

import concourse.bass as bass
from concourse import mybir

F32 = mybir.dt.float32
BF16 = mybir.dt.bfloat16
U32 = mybir.dt.uint32
ALU = mybir.AluOpType
ACT = mybir.ActivationFunctionType
AX = mybir.AxisListType

B, N, D = 16, 512, 128
P = 128
NT = N // P
AH, AD = 16, 8
NG = AH // 2
BZ = 64
NBK = N // BZ
FH, FD = 8, 16
NE, HID = 16, 64
NTILE = NE * HID // P
EPS = 1e-5
SCALE = float(AD) ** -0.5
TERMS = [(0, 0), (0, 1), (0, 2), (1, 0), (1, 1), (2, 0)]
HEAD_DMAS = 2 * len(TERMS)
MXR = NG * NBK // 2
QK_ROWS = len(TERMS) * AD
HALF = 64
FFN_ROWS = len(TERMS) * FD
GATE_ROWS = 3 * NE
BIG = 3.0e38
HEAD_ORDER = [0, 2, 4, 6, 1, 3, 5, 7]
GROUPS = FH * NTILE // 2
G_RING = 8

UNITS = [[(0, 0), (1, 128), (7, 320), (2, 512), (3, 768)], [(4, 0), (5, 256), (6, 512)]]
UNIT_WIDTH = [1024, 768]
PAIR_WIDTH = sum(UNIT_WIDTH)


def query_runs(m):
    if m < 3:
        return [(0, BZ * (m + 2))]
    last = min(m + 1, NBK - 1)
    return [(0, BZ), (BZ * (m - 1), BZ * (last - m + 2))]


def key_range(i):
    if i == 0:
        return 0, N
    return BZ * (i - 1), BZ * min(i + 2, NBK)


CHUNKS = [[(0, 0)], [(1, 0), (2, 192), (7, 384)], [(3, 0), (4, 192)], [(5, 0), (6, 192)]]
REDUCES = [[(0, 0, 1, 512)], [(1, 0, 2, 192), (7, 384, 1, 128)], [(3, 0, 2, 192)], [(5, 0, 2, 192)]]
FIRST_CHUNK = 5
MAX_AT = (18, GROUPS - 3)
SECOND_AT = [5 + 28 * n // 15 for n in range(2 * FH)]
TURN_O_AT, TURN_BACK_AT, OUT_AT = 5, 6, 9
STATS_AT, NORM_AT = 12, 17
TURN_AT = GROUPS - 4
T_AT, Q_AT, K_AT = GROUPS - 2, GROUPS - 1, GROUPS
STEPS = GROUPS + 2
OUT_S, CHUNK_S, GATES_S = 1, 2 * NG + 2, 1
OUT_C, CHUNK_C, SUM_C = 3, 2 * NG, 1


def chunks_at(gi):
    here = [k for k in range(4 * NG) if FIRST_CHUNK + 3 * k // 4 == gi]
    return here[:1], here[1:]


BEFORE_OUT_C = (sum(k % 2 for gi in range(OUT_AT) for part in chunks_at(gi) for k in part) +
                sum(k % 2 for k in chunks_at(OUT_AT)[0]))


class Count:

    def __init__(self):
        self.base, self.n = 0, 0

    def up(self, k=1):
        self.n += k
        return self.base + self.n

    @property
    def now(self):
        return self.base + self.n


def over_batches(eng, counts, prologue, body):
    prologue()
    before = [c.n for c in counts]
    body(0, True, True)
    per = [c.n - k for c, k in zip(counts, before)]
    with eng.Fori(1, B - 2, 1) as b:
        for c, k, p in zip(counts, before, per):
            c.base, c.n = b * p + k, 0
        body(b, True, True)
    for c, k, p in zip(counts, before, per):
        c.base, c.n = (B - 2) * p + k, 0
    body(B - 2, True, False)
    body(B - 1, False, False)


def wait(eng, sem, value):
    if not (isinstance(value, int) and value <= 0):
        eng.wait_ge(sem, value)


def program(nc, x, wq, bq, wk, bk, wv, bv, wo_a, wm, bm, emb, w1b1, w2, b2, wo_f, bo_a, bo_f,
            ident_d, gate_spread_d, head_sum_d, rank_d, minus_d, out):
    with ExitStack() as ctx:
        def sb(name, shape, dt=F32):
            return ctx.enter_context(nc.sbuf_tensor(name, shape, dt))

        def ps(name, shape):
            return ctx.enter_context(nc.psum_tensor(name, shape, F32))

        def sem(name):
            return ctx.enter_context(nc.semaphore(name))

        wq_sb, wk_sb, wv_sb, wm_sb, woa_sb, wof_sb = (sb(n, [P, D]) for n in ("wq", "wk", "wv", "wm", "woa", "wof"))
        bias3 = sb("bias3", [P, 3])
        bq_scaled = sb("bq_scaled", [P, 1])
        bv_sb = sb("bv", [P, D])
        bo_sb = sb("bo", [P, D])
        emb_sb = sb("emb", [P, P])
        arena = sb("arena", [P, 2 * G_RING * 2 * N])
        hid = arena[:, 0:G_RING * 2 * N].rearrange("p (r a n) -> p r a n", a=2, n=N)
        gated = arena[:, G_RING * 2 * N:].rearrange("p (h n) -> p h n", n=N)
        prob_half = [arena[:, h * G_RING * 2 * N:h * G_RING * 2 * N + 4 * PAIR_WIDTH].rearrange(
            "p (g w) -> p g w", g=4) for h in range(2)]
        w1raw = arena[0:FD + 1, 0:NE * HID]
        w1tmp = arena[0:FD + 1, NE * HID:2 * NE * HID]
        w1parts = arena[0:FD + 1, 2 * NE * HID:4 * NE * HID].bitcast(BF16)[:, 0:3 * NE * HID].rearrange(
            "p (c n) -> p c n", c=3)
        bo_two = gated[:, 2 * FH - 1, 0:2 * D].rearrange("p (k d) -> p k d", k=2)
        w1_st = sb("w1_st", [FFN_ROWS + 3, NE * HID], BF16)
        w2_sb = sb("w2", [P, NTILE, 32])
        b2_sb = sb("b2", [P, P])
        ident = sb("ident", [P, P])
        gate_spread = sb("gate_spread", [P, 4, P], BF16)
        head_sum = sb("head_sum", [P, 2, 32])
        rank = sb("rank", [P, NT * FH * NE])
        minus_half = sb("minus_half", [P, NT])

        xt = sb("xt", [P, NT, D])
        idle = sb("idle", [P, 1])
        zero_col = sb("zero_col", [P, 1])
        stats = sb("stats", [P, NT, 6])
        mean_var = sb("mean_var", [P, NT, 2])
        var_eps = sb("var_eps", [P, NT])
        rstd = sb("rstd", [P, NT])
        xn = sb("xn", [P, NT, D])
        xnT = sb("xnT", [P, N])
        q32, k32, t32, gT32 = (sb(n, [P, N]) for n in ("q32", "k32", "t32", "gT32"))
        qk_tmp = sb("qk_tmp", [P, N])
        q_parts, k_parts, t_parts, g_parts = (sb(n, [P, 3, N], BF16) for n in
                                              ("q_parts", "k_parts", "t_parts", "g_parts"))
        k_turned = sb("k_turned", [P, 3, N], BF16)
        rt = [P, NT * FH * NE]
        z, pz, c1, z2 = (sb(n, rt) for n in ("z", "pz", "c1", "z2"))
        gates = sb("gates", [P, 2, N])
        one1, one2 = gates[:, 0, :], gates[:, 1, :]
        dve_tmp = z2
        top = sb("top", [P, 8, NT * FH])

        t_st = sb("t_st", [FFN_ROWS + 3, FH, N], BF16)
        g_st = sb("g_st", [P, FH // 2, N], BF16)
        q_st = sb("q_st", [P, NG, N], BF16)
        q_ch = sb("q_ch", [P, NG, N], BF16)
        k_st = sb("k_st", [P, 2, NG, N], BF16)
        k_dg = sb("k_dg", [P, NG, 2 * N], BF16)
        v_dg = sb("v_dg", [P, NBK, NG, 32])

        mx = [sb(f"mx{h}", [P, P]) for h in range(2)]
        mT32, m_tmp = sb("mT32", [MXR, P]), sb("m_tmp", [MXR, P])
        m_parts = sb("m_parts", [MXR, 2, 3, P], BF16)
        combT = sb("combT", [P, N])
        o_sb = sb("o_sb", [P, 2, N])
        rden = sb("rden", [P, 2, NT * 8])
        o_tok = sb("o_tok", [P, NT, D])
        oT = sb("oT", [P, N])
        xr = sb("xr", [P, NT, D])
        y = sb("y", [P, NT, D])

        ring = ps("ring", [P, 2, 2, N])
        u_bank, g_bank, s_bank, c_bank = (ps(n, [P, N]) for n in ("u_bank", "g_bank", "s_bank", "c_bank"))

        const_in = sem("const_in")
        made = sem("made")
        w1_split = sem("w1_split")
        w1_in = sem("w1_in")
        x_in, xr_in = sem("x_in"), sem("xr_in")
        var_ready, rstd_ready, xn_ready = sem("var_ready"), sem("rstd_ready"), sem("xn_ready")
        q_split, k_split = sem("q_split"), sem("k_split")
        t_split, g_split, m_split = sem("t_split"), sem("g_split"), sem("m_split")
        t_in, g_in, q_in, qc_in, k_in, m_in = (sem(n) for n in ("t_in", "g_in", "q_in", "qc_in", "k_in", "m_in"))
        pz_ready = sem("pz_ready")
        gate_ready = sem("gate_ready")
        v_ready = sem("v_ready")
        ring_full, ring_free = sem("ring_full"), sem("ring_free")
        u_full, u_free = sem("u_full"), sem("u_free")
        g_full, g_free = sem("g_full"), sem("g_free")
        s_full, s_free = sem("s_full"), sem("s_free")
        c_full, c_free = sem("c_full"), sem("c_free")
        hid_ready, prob_ready = sem("hid_ready"), sem("prob_ready")
        k_turn, kd_in, halves_added = sem("k_turn"), sem("kd_in"), sem("halves_added")
        xb_ready, y_out = sem("xb_ready"), sem("y_out")
        dve_done, act_done, pool_done = sem("dve_done"), sem("act_done"), sem("pool_done")

        x_rows = x.rearrange("(b t p) d -> b p t d", p=P, t=NT)
        out_rows = out.rearrange("(b t p) d -> b p t d", p=P, t=NT)

        loads = [
            (wm_sb[:, :], wm), (ident[:, :], ident_d), (wq_sb[:, :], wq), (wk_sb[:, :], wk),
            (bias3[:, 0:1], bq), (bias3[:, 1:2], bk), (bias3[:, 2:3], bm), (emb_sb[:, :], emb),
            (w1raw[:, :], w1b1), (rank[:, :], rank_d.broadcast_to([P, NT * FH * NE])),
            (wv_sb[:, :], wv), (bv_sb[:, :], bv.broadcast_to([P, D])),
            (w2_sb[:, :, :], w2), (b2_sb[:, :], b2), (gate_spread[:, :, :], gate_spread_d),
            (head_sum[:, :, :], head_sum_d),
            (wof_sb[:, :], wo_f), (woa_sb[:, :], wo_a),
            (bo_two[:, 0, :], bo_a.broadcast_to([P, D])), (bo_two[:, 1, :], bo_f.broadcast_to([P, D])),
        ]
        N_MADE = 9

        block = ctx.enter_context(nc.Block())

        @block.sync
        def _(sp):
            x_used, xr_used, c_seen, ring_seen = Count(), Count(), Count(), Count()
            q_s, k_s, t_s, g_s, m_s = Count(), Count(), Count(), Count(), Count()
            counts = [x_used, xr_used, c_seen, ring_seen, q_s, k_s, t_s, g_s, m_s]

            def load_x(b):
                wait(sp, xn_ready, x_used.now)
                x_used.up()
                sp.dma_start(xt[:, :, :], x_rows[b]).then_inc(x_in, 16)

            def restack_t():
                sp.wait_ge(t_split, t_s.up())
                for s, (part, _) in enumerate(TERMS):
                    sp.dma_start(t_st[FD * s:FD * (s + 1), :, :], t_parts[:, part, :]).then_inc(t_in, 16)

            def stack_q(stacked, done):
                for ab in range(2):
                    for s, (part, _) in enumerate(TERMS):
                        r = HALF * ab + AD * s
                        sp.dma_start(stacked[r:r + AD, :, :],
                                     q_parts[HALF * ab:HALF * (ab + 1), part, :]).then_inc(done, 16)

            def stack_k(ab):
                for s, (_, part) in enumerate(TERMS):
                    r = HALF * ab + AD * s
                    sp.dma_start(k_st[r:r + AD, ab, :, :],
                                 k_parts[HALF * ab:HALF * (ab + 1), part, :]).then_inc(k_in, 16)

            def restack_chunks():
                sp.wait_ge(q_split, q_s.up())
                stack_q(q_ch, qc_in)
                sp.wait_ge(k_split, k_s.up())
                stack_k(0)
                restack_g()
                stack_k(1)

            def restack_g():
                sp.wait_ge(g_split, g_s.up())
                for ab in range(2):
                    for part in range(3):
                        r = HALF * ab + NE * part
                        sp.dma_start(g_st[r:r + NE, :, :],
                                     g_parts[HALF * ab:HALF * (ab + 1), part, :]).then_inc(g_in, 16)

            def restack_q():
                wait(sp, ring_full, ring_seen.now)
                stack_q(q_st, q_in)
                sp.wait_ge(k_turn, k_s.now)
                for ab in range(2):
                    for s, (_, part) in enumerate(TERMS):
                        r = HALF * ab + AD * s
                        sp.dma_start(k_dg[r:r + AD, :, N * ab:N * (ab + 1)],
                                     k_turned[HALF * ab:HALF * (ab + 1), part, :]).then_inc(kd_in, 16)

            def place_max():
                for h in range(2):
                    sp.wait_ge(m_split, m_s.up())
                    for ab in range(2):
                        for part in range(3):
                            r = HALF * ab + QK_ROWS + part
                            sp.dma_start(q_st[r:r + 1, 4 * h:4 * h + 4, :],
                                         m_parts[:, h, part, HALF * ab:HALF * (ab + 1)]).then_inc(m_in, 16)
                ring_seen.up(GROUPS + 2 * NG)

            def store(b, before):
                sp.wait_ge(c_free, c_seen.up(OUT_C + before))
                sp.dma_start(out_rows[b], y[:, :, :]).then_inc(y_out, 16)

            def prologue():
                load_x(0)
                for dst, src in loads:
                    sp.dma_start(dst, src).then_inc(const_in, 16)
                sp.wait_ge(made, N_MADE)
                for ab in range(2):
                    r = HALF * ab + QK_ROWS
                    sp.dma_start(k_dg[r:r + 3, :, N * ab:N * (ab + 1)], minus_d).then_inc(w1_in, 16)
                sp.wait_ge(w1_split, 1)
                for s, (_, part) in enumerate(TERMS):
                    sp.dma_start(w1_st[FD * s:FD * (s + 1), :], w1parts[0:FD, part, :]).then_inc(w1_in, 16)
                for part in range(3):
                    r = FFN_ROWS + part
                    sp.dma_start(w1_st[r:r + 1, :], w1parts[FD:FD + 1, part, :]).then_inc(w1_in, 16)
                load_x(1)
                restack_t()
                restack_chunks()
                restack_q()
                place_max()
                c_seen.up(3 + CHUNK_C + 3)

            def body(b, more, more2):
                if more2:
                    load_x(b + 2)
                wait(sp, xb_ready, xr_used.now)
                xr_used.up()
                sp.dma_start(xr[:, :, :], x_rows[b]).then_inc(xr_in, 16)
                if more:
                    restack_t()
                    restack_chunks()
                    restack_q()
                c_seen.up(SUM_C)
                store(b, BEFORE_OUT_C if more else 0)
                if more:
                    place_max()
                    c_seen.up(CHUNK_C - BEFORE_OUT_C + (3 if more2 else 0))

            over_batches(sp, counts, prologue, body)
            sp.wait_ge(y_out, 16 * B)

        @block.gpsimd
        def _(pool):
            step = Count()
            var_s, q_s, k_s, xr_s, q_in_s, k_in_s, c_s, kd_in_s, u_s, y_s, qc_in_s = (Count() for _ in range(11))
            counts = [step, var_s, q_s, k_s, xr_s, q_in_s, k_in_s, c_s, kd_in_s, u_s, y_s, qc_in_s]

            def link(ins):
                ins.then_inc(pool_done, 1)
                pool.wait_ge(pool_done, step.up())

            def power():
                pool.wait_ge(var_ready, var_s.up())
                nc.gpsimd.tensor_tensor(rstd[:, :], var_eps[:, :], minus_half[:, :], ALU.pow).then_inc(rstd_ready, 1)

            zeros = zero_col[:, :].broadcast_to([P, N])

            def split(src, parts, done):
                link(nc.gpsimd.tensor_tensor(parts[:, 0, :], src, zeros, ALU.add))
                link(nc.gpsimd.tensor_tensor(qk_tmp[:, :], src, parts[:, 0, :], ALU.subtract))
                link(nc.gpsimd.tensor_tensor(parts[:, 1, :], qk_tmp[:, :], zeros, ALU.add))
                nc.gpsimd.tensor_tensor(parts[:, 2, :], qk_tmp[:, :], parts[:, 1, :], ALU.subtract).then_inc(done, 1)

            def split_qk():
                wait(pool, q_in, q_in_s.now)
                q_in_s.up(HEAD_DMAS * 16)
                wait(pool, qc_in, qc_in_s.now)
                qc_in_s.up(HEAD_DMAS * 16)
                pool.wait_ge(c_free, c_s.up())
                split(q32[:, :], q_parts, q_split)
                pool.wait_ge(q_split, q_s.up())
                wait(pool, k_in, k_in_s.now)
                k_in_s.up(HEAD_DMAS * 16)
                pool.wait_ge(c_free, c_s.up())
                split(k32[:, :], k_parts, k_split)
                pool.wait_ge(k_split, k_s.up())
                wait(pool, kd_in, kd_in_s.now)
                kd_in_s.up(HEAD_DMAS * 16)
                for part in range(3):
                    ins = nc.gpsimd.tensor_tensor(
                        k_turned[:, part, :].rearrange("p (k m) -> p m k", m=NBK),
                        k_parts[:, part, :].rearrange("p (m k) -> p m k", m=NBK),
                        zero_col[:, :].unsqueeze(2).broadcast_to([P, NBK, BZ]), ALU.add)
                ins.then_inc(k_turn, 1)

            def gelu_phase(early):
                for j in range(FH):
                    pool.wait_ge(u_free, u_s.up(2))
                    nc.gpsimd.tensor_tensor(gated[:, 2 * j, :], gated[:, 2 * j, :], gated[:, 2 * j + 1, :],
                                            ALU.add).then_inc(halves_added, 1)
                    if early and j == 1:
                        power()
                c_s.up(CHUNK_C + (1 if early else 0))

            def prologue():
                nc.gpsimd.memset(zero_col[:, :], 0.0).then_inc(made, 1)
                nc.gpsimd.memset(minus_half[:, :], -0.5).then_inc(made, 1)
                nc.gpsimd.memset(q_st[:, :, :].bitcast(U32), 0).then_inc(made, 1)
                nc.gpsimd.memset(q_ch[:, :, :].bitcast(U32), 0).then_inc(made, 1)
                nc.gpsimd.memset(k_st[:, :, :, :].bitcast(U32), 0).then_inc(made, 1)
                nc.gpsimd.memset(k_dg[:, :, :].bitcast(U32), 0).then_inc(made, 1)
                pool.wait_ge(const_in, 16 * len(loads))
                pool.wait_ge(made, N_MADE)
                nc.gpsimd.tensor_tensor(bo_sb[:, :], bo_two[:, 0, :], bo_two[:, 1, :], ALU.add).then_inc(made, 1)
                pool.wait_ge(made, N_MADE + 1)
                power()
                c_s.up()
                split_qk()
                gelu_phase(True)

            def body(b, more, more2):
                if more:
                    split_qk()
                pool.wait_ge(xr_in, xr_s.up(16))
                wait(pool, y_out, y_s.now)
                y_s.up(16)
                for j in range(NT):
                    ins = nc.gpsimd.tensor_tensor(y[:, j, :], xr[:, j, :], bo_sb[:, :], ALU.add)
                ins.then_inc(xb_ready, 1)
                if more:
                    c_s.up(SUM_C + OUT_C)
                    u_s.up()
                    gelu_phase(more2)

            over_batches(pool, counts, prologue, body)

        @block.scalar
        def _(act):
            ring_s, l2_s, g_s, s_s, c_s, o1_s = (Count() for _ in range(6))
            counts = [ring_s, l2_s, g_s, s_s, c_s, o1_s]

            def take_xnT():
                act.wait_ge(s_full, s_s.up())
                nc.scalar.activation(xnT[:, :], s_bank[:, :], ACT.Identity).then_inc(s_free, 1)

            def gate_exp():
                act.wait_ge(s_free, s_s.up())
                nc.scalar.activation(pz[:, :], z[:, :], ACT.Exp).then_inc(pz_ready, 1)

            def take_q():
                act.wait_ge(c_full, c_s.up())
                nc.scalar.activation(q32[:, :], c_bank[:, :], ACT.Identity, bias=bq_scaled[:, :],
                                     scale=SCALE).then_inc(c_free, 1)

            def take_k():
                act.wait_ge(c_full, c_s.up())
                nc.scalar.activation(k32[:, :], c_bank[:, :], ACT.Identity, bias=bias3[:, 1:2]).then_inc(c_free, 1)

            def copy_gates(n):
                act.wait_ge(g_full, g_s.up())
                if n >= 2:
                    act.wait_ge(u_free, l2_s.now + n - 1)
                nc.scalar.activation(gates[:, n % 2, :], g_bank[:, :], ACT.Identity).then_inc(g_free, 1)

            def gelu_phase(early):
                s_s.up(CHUNK_S)
                c_s.up(CHUNK_C)
                for gi in range(STEPS):
                    if gi < GROUPS:
                        act.wait_ge(ring_full, ring_s.up())
                        if gi >= G_RING and gi % 2 == 0:
                            act.wait_ge(u_full, l2_s.now + (gi - G_RING) // 2 + 1)
                        nc.scalar.activation(hid[:, gi % G_RING, :, :], ring[:, gi % 2, :, :],
                                             ACT.Gelu).then_inc(hid_ready, 1)
                    if early and gi == TURN_AT:
                        take_xnT()
                    if gi + 1 in SECOND_AT:
                        copy_gates(SECOND_AT.index(gi + 1))
                    if early and gi == Q_AT:
                        c_s.up()
                        take_q()
                    if early and gi == K_AT:
                        take_k()
                l2_s.up(2 * FH)
                s_s.up()

            def prologue():
                act.wait_ge(const_in, 16 * len(loads))
                nc.scalar.mul(bq_scaled[:, :], bias3[:, 0:1], SCALE).then_inc(act_done, 1)
                act.wait_ge(act_done, 1)
                take_xnT()
                gate_exp()
                s_s.up(GATES_S)
                c_s.up()
                take_q()
                take_k()
                gelu_phase(True)

            def body(b, more, more2):
                for g in range(NG):
                    for n in range(2):
                        act.wait_ge(ring_full, ring_s.up())
                        at = n * UNIT_WIDTH[0]
                        src = ring[:, n, :, :].rearrange("p a n -> p (a n)")[:, 0:UNIT_WIDTH[n]]
                        nc.scalar.activation(prob_half[g // 4][:, g % 4, at:at + UNIT_WIDTH[n]], src,
                                             ACT.Exp).then_inc(prob_ready, 1)
                    if more and g == 1:
                        gate_exp()
                c_s.up(SUM_C)
                if more:
                    s_s.up(GATES_S + OUT_S)
                    c_s.up(OUT_C)
                    l2_s.up()
                    g_s.up()
                    gelu_phase(more2)

            over_batches(act, counts, prologue, body)

        @block.vector
        def _(dve):
            step = Count()
            x_s, r_s, sf, cf, uf, gf, pz_s = (Count() for _ in range(7))
            m_s, t_s, g_s, t_in_s, g_in_s, m_in_s, xb_s, y_s, comb_s, v_s, o_s = (Count() for _ in range(11))
            counts = [step, x_s, r_s, sf, cf, uf, gf, pz_s, m_s, t_s, g_s, t_in_s, g_in_s, m_in_s, xb_s, y_s,
                      comb_s, v_s, o_s]

            def link(ins):
                ins.then_inc(dve_done, 1)
                dve.wait_ge(dve_done, step.up())

            def split(src, parts, tmp, done):
                link(nc.vector.tensor_copy(parts[:, 0, :], src))
                link(nc.vector.tensor_tensor(tmp, src, parts[:, 0, :], ALU.subtract))
                link(nc.vector.tensor_copy(parts[:, 1, :], tmp))
                nc.vector.tensor_tensor(parts[:, 2, :], tmp, parts[:, 1, :], ALU.subtract).then_inc(done, 1)

            def norm_stats():
                dve.wait_ge(x_in, x_s.up(16))
                for j in range(NT):
                    ins = nc.vector.bn_stats(stats[:, j, :], xt[:, j, :])
                link(ins)
                nc.vector.tensor_copy(idle[:, :], bias3[:, 0:1])
                for j in range(NT):
                    ins = nc.vector.bn_aggr(mean_var[:, j, :], stats[:, j, :])
                link(ins)
                nc.vector.tensor_scalar(var_eps[:, :], mean_var[:, :, 1], EPS, None, ALU.add).then_inc(var_ready, 1)

            def normalise():
                dve.wait_ge(rstd_ready, r_s.up())
                for j in range(NT):
                    ins = nc.vector.tensor_scalar(xn[:, j, :], xt[:, j, :], mean_var[:, j, 0:1], rstd[:, j:j + 1],
                                                  ALU.subtract, ALU.mult)
                ins.then_inc(xn_ready, 1)

            def take_t():
                dve.wait_ge(c_full, cf.up())
                nc.vector.tensor_scalar(t32[:, :], c_bank[:, :], bias3[:, 2:3], None, ALU.add).then_inc(c_free, 1)

            def split_t():
                dve.wait_ge(c_free, cf.now)
                wait(dve, t_in, t_in_s.now)
                t_in_s.up(16 * len(TERMS))
                split(t32[:, :], t_parts, dve_tmp[:, :], t_split)
                dve.wait_ge(t_split, t_s.up())

            R = NT * FH // 4

            def by_expert(t):
                return t[:, :].rearrange("p (r e h) -> p r h e", r=R, h=4)

            def per_head(k, spread=True):
                v = top[:, k, :].rearrange("p (r h) -> p r h", h=4)
                return v.unsqueeze(3).broadcast_to([P, R, 4, NE]) if spread else v

            def take_logits():
                dve.wait_ge(s_full, sf.up())
                zp = s_bank[:, :].rearrange("p (r e h) -> p r h e", r=R, h=4)
                link(nc.vector.tensor_reduce(per_head(0, False), zp, AX.X, ALU.max))
                nc.vector.tensor_tensor(by_expert(z), zp, per_head(0), ALU.subtract).then_inc(s_free, 1)

            def route():
                dve.wait_ge(s_free, sf.now)
                for n, (zz, one) in enumerate([(z, one1), (z2, one2)]):
                    if n == 0:
                        link(nc.vector.scalar_tensor_tensor(c1[:, :], z[:, :], 0.0, rank[:, :], ALU.is_equal, ALU.mult))
                    else:
                        link(nc.vector.scalar_tensor_tensor(z2[:, :], one1[:, :], -BIG, z[:, :], ALU.mult, ALU.add))
                        link(nc.vector.tensor_reduce(per_head(1, False), by_expert(z2), AX.X, ALU.max))
                        link(nc.vector.tensor_tensor(by_expert(one2), by_expert(z2), per_head(1), ALU.is_equal))
                        link(nc.vector.tensor_tensor(c1[:, :], one2[:, :], rank[:, :], ALU.mult))
                    link(nc.vector.tensor_reduce(per_head(2 + n, False), by_expert(c1), AX.X, ALU.max))
                    link(nc.vector.tensor_tensor(by_expert(one), by_expert(c1), per_head(2 + n), ALU.is_equal))
                link(nc.vector.tensor_tensor(c1[:, :], one1[:, :], one2[:, :], ALU.add))
                dve.wait_ge(pz_ready, pz_s.up())
                link(nc.vector.tensor_reduce(per_head(4, False), by_expert(pz), AX.X, ALU.add))
                link(nc.vector.reciprocal(top[:, 5, :], top[:, 4, :]))
                link(nc.vector.tensor_tensor(z2[:, :], pz[:, :], c1[:, :], ALU.mult))
                nc.vector.tensor_tensor(by_expert(c1), by_expert(z2), per_head(5), ALU.mult).then_inc(gate_ready, 1)

            def take_gates():
                dve.wait_ge(s_full, sf.up())
                nc.vector.tensor_copy(gT32[:, :], s_bank[:, :]).then_inc(s_free, 1)
                dve.wait_ge(s_free, sf.now)
                wait(dve, g_in, g_in_s.now)
                g_in_s.up(16 * 6)
                split(gT32[:, :], g_parts, dve_tmp[:, :], g_split)
                dve.wait_ge(g_split, g_s.up())

            def take_v():
                dve.wait_ge(s_full, sf.up())
                for ab in range(2):
                    rows = slice(HALF * ab, HALF * (ab + 1))
                    src = s_bank[rows, :].rearrange("p (m g d) -> p m g d", m=NBK, d=AD)
                    bias = bv_sb[rows, HALF * ab:HALF * (ab + 1)].rearrange("p (g d) -> p g d", d=AD)
                    ins = nc.vector.tensor_tensor(v_dg[rows, :, :, 16 * ab:16 * ab + AD], src,
                                                  bias.unsqueeze(1).broadcast_to([HALF, NBK, NG, AD]), ALU.add)
                ins.then_inc(s_free, 1)

            def take_max(g, c):
                bank, full, free, cnt = ((s_bank, s_full, s_free, sf), (c_bank, c_full, c_free, cf))[c % 2]
                dve.wait_ge(full, cnt.up())
                for i, col, n, width in REDUCES[c]:
                    at = g % 4 * NBK + i
                    ins = nc.vector.tensor_reduce(mx[g // 4][:, at:at + n],
                                                  bank[:, col:col + n * width].rearrange("p (n w) -> p n w", n=n),
                                                  AX.X, ALU.max)
                ins.then_inc(free, 1)

            def take_mT(h):
                rows = slice(0, MXR)
                dve.wait_ge(s_full, sf.up())
                nc.vector.tensor_copy(mT32[:, :], s_bank[rows, 0:P]).then_inc(s_free, 1)
                dve.wait_ge(s_free, sf.now)
                wait(dve, m_in, m_in_s.now)
                m_in_s.up(16 * 6)
                split(mT32[:, :], m_parts[:, h, :, :], m_tmp[:, :], m_split)
                dve.wait_ge(m_split, m_s.up())

            def gate_half(n):
                dve.wait_ge(g_free, gf.up())
                dve.wait_ge(u_full, uf.up())
                nc.vector.tensor_tensor(gated[:, n, :], u_bank[:, :], gates[:, n % 2, :], ALU.mult).then_inc(u_free, 1)

            def take_comb():
                dve.wait_ge(c_full, cf.up())
                nc.vector.tensor_copy(combT[:, :], c_bank[:, :]).then_inc(c_free, 1)

            def take_o(grp):
                bank, full, free = ((u_bank, u_full, u_free), (g_bank, g_full, g_free))[grp]
                dve.wait_ge(full, uf.up() if grp == 0 else gf.now)
                nc.vector.tensor_copy(o_sb[:, grp, :], bank[:, :]).then_inc(free, 1)

            def normalise_o(grp):
                bank, full, free, cnt = ((c_bank, c_full, c_free, cf), (s_bank, s_full, s_free, sf))[grp]
                dve.wait_ge(full, cnt.up())
                heads = bank[:, :].rearrange("p (j k r) -> p j k r", j=NT, r=16)
                recip = rden[:, grp, :].rearrange("p (j k) -> p j k", j=NT)
                link(nc.vector.reciprocal(recip, heads[:, :, :, AD]))
                nc.vector.tensor_tensor(o_tok[:, :, HALF * grp:HALF * (grp + 1)].rearrange("p j (k d) -> p j k d", d=AD),
                                        heads[:, :, :, 0:AD], recip.unsqueeze(3).broadcast_to([P, NT, 8, AD]),
                                        ALU.mult).then_inc(free, 1)

            def take_oT():
                dve.wait_ge(c_full, cf.up())
                nc.vector.tensor_copy(oT[:, :], c_bank[:, :]).then_inc(c_free, 1)

            def finish():
                dve.wait_ge(xb_ready, xb_s.up())
                dve.wait_ge(c_full, cf.up())
                row = y[:, :, :].rearrange("p t d -> p (t d)")
                nc.vector.tensor_tensor(row, c_bank[:, :], row, ALU.add).then_inc(c_free, 1)

            def gelu_phase(with_out, early):
                for gi in range(STEPS):
                    if with_out and gi == 0:
                        normalise_o(0)
                    if gi == 3:
                        if with_out:
                            take_o(1)
                        take_v()
                    if with_out and gi == TURN_O_AT:
                        normalise_o(1)
                    if with_out and gi == TURN_BACK_AT:
                        take_oT()
                    if early and gi == STATS_AT:
                        norm_stats()
                    if early and gi == NORM_AT:
                        normalise()
                    if early and gi == TURN_AT:
                        sf.up()
                    first, rest = chunks_at(gi)
                    for chunk in first:
                        take_max(chunk // 4, chunk % 4)
                    if gi in SECOND_AT:
                        gate_half(SECOND_AT.index(gi))
                    if with_out and gi == OUT_AT:
                        finish()
                    for chunk in rest:
                        take_max(chunk // 4, chunk % 4)
                    if gi in MAX_AT:
                        take_mT(MAX_AT.index(gi))
                    if early and gi == T_AT:
                        take_t()

            def prologue():
                nc.vector.memset(t_st[:, :, :], 1.0).then_inc(made, 1)
                nc.vector.memset(g_st[:, :, :].bitcast(U32), 0).then_inc(made, 1)
                nc.vector.memset(v_dg[:, :, :, :], 0.0).then_inc(made, 1)
                nc.vector.memset(mx[0][:, :], 0.0)
                nc.vector.memset(mx[1][:, :], 0.0)
                dve.wait_ge(made, N_MADE)
                for ab in range(2):
                    rows = slice(HALF * ab, HALF * (ab + 1))
                    ins = nc.vector.memset(v_dg[rows, :, :, 16 * ab + AD:16 * ab + AD + 1], 1.0)
                link(ins)
                dve.wait_ge(const_in, 16 * len(loads))
                norm_stats()
                split(w1raw, w1parts, w1tmp, w1_split)
                normalise()
                sf.up()
                take_t()
                split_t()
                take_logits()
                route()
                take_gates()
                cf.up(2)
                gelu_phase(False, True)

            def body(b, more, more2):
                if more:
                    split_t()
                    take_logits()
                    route()
                    cf.up(2)
                take_comb()
                if more:
                    take_gates()
                take_o(0)
                if more:
                    gf.up()
                    gelu_phase(True, more2)
                else:
                    gf.up()
                    normalise_o(0)
                    take_o(1)
                    normalise_o(1)
                    take_oT()
                    finish()

            over_batches(dve, counts, prologue, body)

        @block.tensor
        def _(pe):
            mm = nc.tensor.matmul
            xnT_at, t_at, o1_at = [None], [None], [None]
            xn_s, s_uses, c_uses, u_uses, g_uses, ring_uses = (Count() for _ in range(6))
            gate_s, hid_s, prob_s, added_s, t_in_s, g_in_s, q_s, qc_s, k_s, m_s, kd_s = (Count() for _ in range(11))
            counts = [xn_s, s_uses, c_uses, u_uses, g_uses, ring_uses, gate_s, hid_s, prob_s, added_s, t_in_s, g_in_s,
                      q_s, qc_s, k_s, m_s, kd_s]

            def claim(free, uses):
                wait(pe, free, uses.now)
                uses.up()

            def turn_xn():
                pe.wait_ge(xn_ready, xn_s.up())
                claim(s_free, s_uses)
                for j in range(NT):
                    ins = nc.tensor.transpose(s_bank[:, j * P:(j + 1) * P], xn[:, j, :], ident[:, :])
                ins.then_inc(s_full, 1)
                xnT_at[0] = s_uses.now

            def project_t():
                pe.wait_ge(s_free, xnT_at[0])
                project(wm_sb, c_bank, c_free, c_uses, c_full)
                t_at[0] = c_uses.now

            def project(weight, bank, free, uses, full):
                claim(free, uses)
                mm(bank[:, :], weight[:, :], xnT[:, :], start=True, stop=True).then_inc(full, 1)

            def logits():
                pe.wait_ge(c_free, t_at[0])
                claim(s_free, s_uses)
                for j in range(NT):
                    ins = mm(s_bank[:, j * P:(j + 1) * P], t32[:, j * P:(j + 1) * P], emb_sb[:, :], start=True, stop=True)
                ins.then_inc(s_full, 1)

            def turn_gates():
                pe.wait_ge(gate_ready, gate_s.up())
                claim(s_free, s_uses)
                for j in range(NT):
                    ins = nc.tensor.transpose(s_bank[:, j * P:(j + 1) * P], c1[:, j * P:(j + 1) * P], ident[:, :])
                ins.then_inc(s_full, 1)

            def values():
                claim(s_free, s_uses)
                for m in range(NBK):
                    for ab in range(2):
                        ins = mm(s_bank[HALF * ab:HALF * (ab + 1), m * HALF:(m + 1) * HALF],
                                 xnT[:, m * BZ:(m + 1) * BZ], wv_sb[:, HALF * ab:HALF * (ab + 1)], start=True, stop=True)
                ins.then_inc(s_full, 1)

            def score_chunk(g, c):
                bank, full, free, uses = ((s_bank, s_full, s_free, s_uses), (c_bank, c_full, c_free, c_uses))[c % 2]
                claim(free, uses)
                for i, col in CHUNKS[c]:
                    lo, hi = key_range(i)
                    for ab in range(2):
                        ins = mm(bank[HALF * ab:HALF * (ab + 1), col:col + hi - lo],
                                 q_ch[:, g, i * BZ:(i + 1) * BZ], k_st[:, ab, g, lo:hi], start=True, stop=True)
                ins.then_inc(full, 1)

            def turn_max(h):
                pe.wait_ge(c_free, c_uses.now)
                claim(s_free, s_uses)
                nc.tensor.transpose(s_bank[:, 0:P], mx[h][:, :], ident[:, :]).then_inc(s_full, 1)

            def hidden(gi):
                h = HEAD_ORDER[gi // 4]
                for a in range(2):
                    t = 2 * (gi % 4) + a
                    ins = mm(ring[:, gi % 2, a, :], w1_st[:, t * P:(t + 1) * P], t_st[:, h, :], start=True, stop=True)
                ins.then_inc(ring_full, 1)

            def spread_gates(n):
                h, u = HEAD_ORDER[n // 2], n % 2
                claim(g_free, g_uses)
                mm(g_bank[:, :], gate_spread[0:HALF + GATE_ROWS, 2 * (h % 2) + u, :], g_st[0:HALF + GATE_ROWS, h // 2, :],
                   start=True, stop=True).then_inc(g_full, 1)

            def second(n):
                claim(u_free, u_uses)
                pe.wait_ge(hid_ready, hid_s.now + 2 * (n + 1))
                for a in range(4):
                    t = 4 * (n % 2) + a
                    slot = (2 * n + a // 2) % G_RING
                    ins = mm(u_bank[32 * a:32 * (a + 1), :], w2_sb[:, t, :], hid[:, slot, a % 2, :], start=True, stop=True)
                ins.then_inc(u_full, 1)

            def combine_bias():
                claim(c_free, c_uses)
                mm(c_bank[:, :], b2_sb[:, :], gT32[:, :], start=True, stop=False, skip_group_check=True)

            def combine(group):
                if group == 0:
                    pe.wait_ge(halves_added, added_s.up(FH))
                for q in range(4):
                    ins = mm(c_bank[32 * q:32 * (q + 1), :], head_sum[:, group, :], gated[:, 8 * group + 2 * q, :],
                             start=False, stop=(group == 1), skip_group_check=True)
                if group == 1:
                    ins.then_inc(c_full, 1)

            def shifted(g, n):
                for m, col in UNITS[n]:
                    for lo, width in query_runs(m):
                        bank, c0 = col // N, col % N
                        ins = mm(ring[:, n, bank, c0:c0 + width], k_dg[:, g, m:2 * N:NBK], q_st[:, g, lo:lo + width],
                                 start=True, stop=True)
                        col += width
                ins.then_inc(ring_full, 1)

            def attend(grp, ms):
                if 0 in ms:
                    claim((u_free, g_free)[grp], (u_uses, g_uses)[grp])
                bank = (u_bank, g_bank)[grp]
                for m in ms:
                    for lo, width in query_runs(m):
                        n = next(k for k in range(2) if m in [a for a, _ in UNITS[k]])
                        col = dict(UNITS[n])[m] + n * UNIT_WIDTH[0]
                        off = 0 if lo == 0 else BZ
                        for q in range(4):
                            ins = mm(bank[32 * q:32 * (q + 1), lo:lo + width], v_dg[:, m, 4 * grp + q, :],
                                     prob_half[grp][:, q, col + off:col + off + width],
                                     start=(m == 0), stop=(m == NBK - 1), skip_group_check=True)
                if NBK - 1 in ms:
                    ins.then_inc((u_full, g_full)[grp], 1)

            def turn_o(grp):
                bank, full, free, uses = ((c_bank, c_full, c_free, c_uses), (s_bank, s_full, s_free, s_uses))[grp]
                claim(free, uses)
                pe.wait_ge((u_free, g_free)[grp], (u_uses, g_uses)[grp].now)
                for j in range(NT):
                    ins = nc.tensor.transpose(bank[:, j * P:(j + 1) * P], o_sb[:, grp, j * P:(j + 1) * P], ident[:, :])
                ins.then_inc(full, 1)
                if grp == 1:
                    o1_at[0] = s_uses.now

            def turn_back():
                pe.wait_ge(s_free, o1_at[0])
                claim(c_free, c_uses)
                for j in range(NT):
                    ins = nc.tensor.transpose(c_bank[:, j * P:(j + 1) * P], o_tok[:, j, :], ident[:, :])
                ins.then_inc(c_full, 1)

            def project_out():
                claim(c_free, c_uses)
                for j in range(NT):
                    tok = slice(j * P, (j + 1) * P)
                    mm(c_bank[:, tok], combT[:, tok], wof_sb[:, :], start=True, stop=False)
                    ins = mm(c_bank[:, tok], oT[:, tok], woa_sb[:, :], start=False, stop=True)
                ins.then_inc(c_full, 1)

            def gelu_phase(with_out, early):
                for gi in range(STEPS):
                    if gi < GROUPS:
                        if gi == 0:
                            pe.wait_ge(t_in, t_in_s.up(16 * len(TERMS)))
                        if gi < 2:
                            if with_out:
                                pe.wait_ge(prob_ready, prob_s.now + gi - 1)
                        else:
                            pe.wait_ge(hid_ready, hid_s.now + gi - 1)
                        hidden(gi)
                    if with_out:
                        if gi < 2:
                            attend(1, range(4 * gi, 4 * gi + 4))
                        if gi == 0:
                            turn_o(0)
                    if gi == 3:
                        values()
                    if with_out:
                        if gi == TURN_O_AT:
                            turn_o(1)
                        if gi == TURN_BACK_AT:
                            turn_back()
                    if gi == SECOND_AT[0] - 1:
                        pe.wait_ge(g_in, g_in_s.up(16 * 6))
                    if gi == FIRST_CHUNK:
                        pe.wait_ge(qc_in, qc_s.up(16 * HEAD_DMAS))
                        pe.wait_ge(k_in, k_s.up(16 * HEAD_DMAS))
                    if early and gi == TURN_AT:
                        turn_xn()
                    first, rest = chunks_at(gi)
                    for chunk in first:
                        score_chunk(chunk // 4, chunk % 4)
                    if gi in SECOND_AT:
                        second(SECOND_AT.index(gi))
                    if gi + 1 in SECOND_AT:
                        spread_gates(SECOND_AT.index(gi + 1))
                    if with_out and gi == OUT_AT:
                        project_out()
                    for chunk in rest:
                        score_chunk(chunk // 4, chunk % 4)
                    if gi in MAX_AT:
                        turn_max(MAX_AT.index(gi))
                    if early and gi == T_AT:
                        project_t()
                    if early and gi == Q_AT:
                        project(wq_sb, c_bank, c_free, c_uses, c_full)
                    if early and gi == K_AT:
                        project(wk_sb, c_bank, c_free, c_uses, c_full)
                hid_s.up(GROUPS)

            def prologue():
                pe.wait_ge(const_in, 16 * len(loads))
                pe.wait_ge(made, N_MADE)
                turn_xn()
                project_t()
                logits()
                project(wq_sb, c_bank, c_free, c_uses, c_full)
                project(wk_sb, c_bank, c_free, c_uses, c_full)
                turn_gates()
                pe.wait_ge(w1_in, 16 * 11)
                gelu_phase(False, True)

            def body(b, more, more2):
                pe.wait_ge(q_in, q_s.up(16 * HEAD_DMAS))
                pe.wait_ge(kd_in, kd_s.up(16 * HEAD_DMAS))
                for g in range(NG):
                    if g % 4 == 0:
                        pe.wait_ge(m_in, m_s.up(16 * 6))
                    for n in range(2):
                        if g == 0:
                            pe.wait_ge(hid_ready, hid_s.now + n - 1)
                        else:
                            pe.wait_ge(prob_ready, prob_s.now + 2 * g + n - 1)
                        shifted(g, n)
                    if g == 0:
                        if more:
                            logits()
                        combine_bias()
                    if g in (1, 2):
                        combine(g - 1)
                    if g >= 4:
                        if g == 4:
                            pe.wait_ge(prob_ready, prob_s.now + 8)
                        attend(0, [2 * (g - 4), 2 * (g - 4) + 1])
                    if more and g == 6:
                        turn_gates()
                prob_s.up(2 * NG)
                if more:
                    gelu_phase(True, more2)
                else:
                    pe.wait_ge(prob_ready, prob_s.now)
                    attend(1, range(NBK))
                    turn_o(0)
                    turn_o(1)
                    turn_back()
                    project_out()

            over_batches(pe, counts, prologue, body)


def kernel(**inputs):
    import ml_dtypes as _ml
    import numpy as _np
    import concourse.bacc as _bacc
    from concourse import mybir as _mybir
    from concourse.bass_utils import run_bass_kernel_spmd as _run

    a = {k: _np.asarray(v) for k, v in inputs.items()}
    f32 = _np.float32

    def pair_cols(w):
        return w.reshape(-1, NG, 2, AD).transpose(0, 2, 3, 1).reshape(-1, D)

    wv = a["L0_attn_Wv"].reshape(D, NG, 2, AD).transpose(0, 2, 1, 3).reshape(D, D)
    bv = a["L0_attn_bv"].reshape(NG, 2, AD).transpose(1, 0, 2).reshape(1, D)
    wm = a["L0_ffn_Wm"].reshape(D, FH, FD).transpose(0, 2, 1).reshape(D, D)
    bm = a["L0_ffn_bm"].reshape(FH, FD).T.reshape(D, 1)
    emb = _np.zeros((FD, FH // 2, 2, 2, NE, FH // 2), f32)
    b2 = _np.zeros((2, NE, FH // 2, FH // 2, 2, FD), f32)
    for hp in range(FH // 2):
        for ab in range(2):
            emb[:, hp, ab, ab, :, hp] = a["L0_ffn_expert_emb"]
            b2[ab, :, hp, hp, ab, :] = a["L0_ffn_b2"]
    w1b1 = _np.concatenate([a["L0_ffn_W1"].transpose(1, 0, 2).reshape(FD, NE * HID),
                            a["L0_ffn_b1"].reshape(1, NE * HID)])
    w2 = _np.zeros((2, HID, NTILE, 2, FD), f32)
    for k in range(2):
        w2[k, :, :, k, :] = a["L0_ffn_W2"].reshape(NTILE, 2, HID, FD)[:, k].transpose(1, 0, 2)
    gate_spread = _np.zeros((2, HALF, 2, 2, NE // 2, FD), _ml.bfloat16)
    for ab in range(2):
        for part in range(3):
            for e in range(NE):
                gate_spread[ab, NE * part + e, ab, e // 8, e % 8, :] = 1
    head_sum = _np.zeros((NE // 2, FD, 2, 2, FD), f32)
    for o in range(FD):
        for ab in range(2):
            head_sum[:, o, ab, ab, o] = 1
    arrays = {
        "x": a["L0_attn_x"].reshape(B * N, D),
        "wq": pair_cols(a["L0_attn_Wq"]), "bq": pair_cols(a["L0_attn_bq"]).reshape(D, 1),
        "wk": pair_cols(a["L0_attn_Wk"]), "bk": pair_cols(a["L0_attn_bk"]).reshape(D, 1),
        "wv": wv, "bv": bv, "wo_a": a["L0_attn_Wo"], "wm": wm, "bm": bm,
        "emb": emb.reshape(P, P), "w1b1": w1b1, "w2": w2.reshape(P, NTILE, 32), "b2": b2.reshape(P, P),
        "wo_f": a["L0_ffn_Wo"], "bo_a": a["L0_attn_bo"].reshape(1, D), "bo_f": a["L0_ffn_bo"].reshape(1, D),
        "ident": _np.eye(P, dtype=f32), "gate_spread": gate_spread.reshape(P, 4, P),
        "head_sum": head_sum.reshape(P, 2, 32),
        "rank": _np.tile(_np.repeat(_np.arange(NE, 0, -1, dtype=f32), FH // 2), 2 * NT).reshape(1, NT * FH * NE),
        "minus": _np.full((3, NG * N), -1, _ml.bfloat16),
    }
    nc = _bacc.Bacc("TRN2", target_bir_lowering=False, num_devices=1)
    feed, args = {}, []
    for name, v in arrays.items():
        v = _np.ascontiguousarray(v)
        feed[f"in_{name}"] = v
        args.append(nc.dram_tensor(f"in_{name}", v.shape, _mybir.dt.from_np(v.dtype), kind="ExternalInput").ap())
    args.append(nc.dram_tensor("out_0", (B * N, D), _mybir.dt.from_np(_np.dtype("float32")), kind="ExternalOutput").ap())
    program(nc, *args)
    r = _run(nc, [feed], core_ids=[0])
    return r.results[0]["out_0"].reshape(B, N, D)
```

```python
from contextlib import ExitStack

import concourse.bass as bass
from concourse import mybir

F32 = mybir.dt.float32
BF16 = mybir.dt.bfloat16
U32 = mybir.dt.uint32
ALU = mybir.AluOpType
ACT = mybir.ActivationFunctionType
AX = mybir.AxisListType

B, N, D = 16, 512, 128
P = 128
NT = N // P
AH, AD = 16, 8
NG = AH // 2
BZ = 64
NBK = N // BZ
FH, FD = 8, 16
NE, HID = 16, 64
NTILE = NE * HID // P
EPS = 1e-5
SCALE = float(AD) ** -0.5
TERMS = [(0, 0), (0, 1), (0, 2), (1, 0), (1, 1), (2, 0)]
Q_DMAS, K_DMAS = len(TERMS), 2 * len(TERMS)
MXR = NG * NBK // 2
QK_ROWS = len(TERMS) * 2 * AD
HALF = 64
FFN_ROWS = len(TERMS) * FD
GATE_ROWS = 3 * 2 * NE
BIG = 3.0e38
HEAD_ORDER = [0, 2, 4, 6, 1, 3, 5, 7]
GROUPS = FH * NTILE // 2
G_RING = 8

UNITS = [[(0, 0), (1, 128), (7, 320), (2, 512), (3, 768)], [(4, 0), (5, 256), (6, 512)]]
UNIT_WIDTH = [1024, 768]
PAIR_WIDTH = sum(UNIT_WIDTH)


def query_runs(m):
    if m < 3:
        return [(0, BZ * (m + 2))]
    last = min(m + 1, NBK - 1)
    return [(0, BZ), (BZ * (m - 1), BZ * (last - m + 2))]


def key_range(i):
    if i == 0:
        return 0, N
    return BZ * (i - 1), BZ * min(i + 2, NBK)


CHUNKS = [[(0, 0)], [(1, 0), (2, 192), (7, 384)], [(3, 0), (4, 192)], [(5, 0), (6, 192)]]
REDUCES = [[(0, 0, 1, 512)], [(1, 0, 2, 192), (7, 384, 1, 128)], [(3, 0, 2, 192)], [(5, 0, 2, 192)]]
FIRST_CHUNK = 6
MAX_AT = (20, GROUPS - 1)
SECOND_AT = [5 + 27 * n // 15 for n in range(2 * FH)]
VALUES_AT, TURN_O_AT, TURN_BACK_AT, OUT_AT = 2, 4, 5, 8
STATS_AT, NORM_AT = 9, 15
TURN_AT = GROUPS - 3
T_AT, Q_AT = GROUPS - 2, GROUPS - 1
OUT_S, CHUNK_S, GATES_S = 1, 2 * NG + 2, 1
OUT_C, CHUNK_C, SUM_C = 3, 2 * NG, 1


def chunks_at(gi):
    here = [k for k in range(4 * NG) if FIRST_CHUNK + 3 * k // 4 == gi]
    return here[:1], here[1:]


BEFORE_OUT_C = (sum(k % 2 for gi in range(OUT_AT) for part in chunks_at(gi) for k in part) +
                sum(k % 2 for k in chunks_at(OUT_AT)[0]))


class Count:

    def __init__(self):
        self.base, self.n = 0, 0

    def up(self, k=1):
        self.n += k
        return self.base + self.n

    @property
    def now(self):
        return self.base + self.n


def over_batches(eng, counts, prologue, body):
    prologue()
    before = [c.n for c in counts]
    body(0, True, True)
    per = [c.n - k for c, k in zip(counts, before)]
    with eng.Fori(1, B - 2, 1) as b:
        for c, k, p in zip(counts, before, per):
            c.base, c.n = b * p + k, 0
        body(b, True, True)
    for c, k, p in zip(counts, before, per):
        c.base, c.n = (B - 2) * p + k, 0
    body(B - 2, True, False)
    body(B - 1, False, False)


def wait(eng, sem, value):
    if not (isinstance(value, int) and value <= 0):
        eng.wait_ge(sem, value)


def program(nc, x, first, weights, rows, biases, w1b1, gate_spread_d, minus_d, out):
    with ExitStack() as ctx:
        def sb(name, shape, dt=F32):
            return ctx.enter_context(nc.sbuf_tensor(name, shape, dt))

        def ps(name, shape):
            return ctx.enter_context(nc.psum_tensor(name, shape, F32))

        def sem(name):
            return ctx.enter_context(nc.semaphore(name))

        first_sb = sb("first", [P, 3 * D + 3])
        ident, wm_sb, emb_sb = (first_sb[:, k * D:(k + 1) * D] for k in range(3))
        bias3 = first_sb[:, 3 * D:]
        weights_sb = sb("weights", [P, 6 * D + NTILE * 32 + 64])
        wq_sb, wk_sb, wv_sb, woa_sb, wof_sb, b2_sb = (weights_sb[:, k * D:(k + 1) * D] for k in range(6))
        w2_sb = weights_sb[:, 6 * D:6 * D + NTILE * 32].rearrange("p (t o) -> p t o", o=32)
        head_sum = weights_sb[:, 6 * D + NTILE * 32:].rearrange("p (k o) -> p k o", o=32)
        rows_sb = sb("rows", [P, NT * FH * NE + D])
        rank, bv_sb = rows_sb[:, 0:NT * FH * NE], rows_sb[:, NT * FH * NE:]
        bq_scaled = sb("bq_scaled", [P, 1])
        bo_sb = sb("bo", [P, D])
        arena = sb("arena", [P, 2 * G_RING * 2 * N])
        hid = arena[:, 0:G_RING * 2 * N].rearrange("p (r a n) -> p r a n", a=2, n=N)
        gated = arena[:, G_RING * 2 * N:].rearrange("p (h n) -> p h n", n=N)
        prob_half = [arena[:, h * G_RING * 2 * N:h * G_RING * 2 * N + 4 * PAIR_WIDTH].rearrange(
            "p (g w) -> p g w", g=4) for h in range(2)]
        w1raw = arena[0:FD + 1, 0:NE * HID]
        w1tmp = arena[0:FD + 1, NE * HID:2 * NE * HID]
        w1parts = arena[0:FD + 1, 2 * NE * HID:4 * NE * HID].bitcast(BF16)[:, 0:3 * NE * HID].rearrange(
            "p (c n) -> p c n", c=3)
        bo_two = gated[:, 2 * FH - 1, 0:2 * D]
        w1_st = sb("w1_st", [FFN_ROWS + 3, NE * HID], BF16)
        gate_spread = sb("gate_spread", [GATE_ROWS, 4, P], BF16)
        minus_half = sb("minus_half", [P, NT])

        xt = sb("xt", [P, NT, D])
        idle = sb("idle", [P, 1])
        zero_col = sb("zero_col", [P, 1])
        stats = sb("stats", [P, NT, 6])
        mean_var = sb("mean_var", [P, NT, 2])
        var_eps = sb("var_eps", [P, NT])
        rstd = sb("rstd", [P, NT])
        xn = sb("xn", [P, NT, D])
        xnT = sb("xnT", [P, N])
        q32, k32, t32, gT32 = (sb(n, [P, N]) for n in ("q32", "k32", "t32", "gT32"))
        qk_tmp = sb("qk_tmp", [P, N])
        q_parts, k_parts, t_parts, g_parts = (sb(n, [P, 3, N], BF16) for n in
                                              ("q_parts", "k_parts", "t_parts", "g_parts"))
        k_turned = sb("k_turned", [P, 3, N], BF16)
        rt = [P, NT * FH * NE]
        z, pz, c1, z2 = (sb(n, rt) for n in ("z", "pz", "c1", "z2"))
        gates = sb("gates", [P, 2, N])
        one1, one2 = gates[:, 0, :], gates[:, 1, :]
        dve_tmp = z2
        top = sb("top", [P, 8, NT * FH])

        t_st = sb("t_st", [FFN_ROWS + 3, FH, N], BF16)
        g_st = sb("g_st", [GATE_ROWS, FH // 2, N], BF16)
        q_st = sb("q_st", [QK_ROWS + 6, NG, N], BF16)
        q_ch = sb("q_ch", [QK_ROWS, NG, N], BF16)
        k_st = sb("k_st", [QK_ROWS, 2, NG, N], BF16)
        k_dg = sb("k_dg", [QK_ROWS + 6, NG, 2 * N], BF16)
        v_dg = sb("v_dg", [P, NBK, NG, 32])

        mx = [sb(f"mx{h}", [P, P]) for h in range(2)]
        m_tmp = sb("m_tmp", [MXR, P])
        m_parts = sb("m_parts", [MXR, 2, 3, P], BF16)
        combT = sb("combT", [P, N])
        o_sb = sb("o_sb", [P, 2, N])
        rden = sb("rden", [P, 2, NT * 8])
        o_tok = sb("o_tok", [P, NT, D])
        oT = sb("oT", [P, N])
        xr = sb("xr", [P, NT, D])
        y = sb("y", [P, NT, D])

        ring = ps("ring", [P, 2, 2, N])
        u_bank, g_bank, s_bank, c_bank = (ps(n, [P, N]) for n in ("u_bank", "g_bank", "s_bank", "c_bank"))

        first_in, w1raw_in, rows_in, const_in = (sem(n) for n in ("first_in", "w1raw_in", "rows_in", "const_in"))
        made = sem("made")
        w1_split = sem("w1_split")
        w1_in = sem("w1_in")
        x_in, xr_in = sem("x_in"), sem("xr_in")
        var_ready, rstd_ready, xn_ready = sem("var_ready"), sem("rstd_ready"), sem("xn_ready")
        t_split, q_split, k_split = sem("t_split"), sem("q_split"), sem("k_split")
        k_turn = sem("k_turn")
        g_split, m_split = sem("g_split"), sem("m_split")
        t_in, g_in, q_in, qc_in, k_in, kd_in, m_in = (sem(n) for n in (
            "t_in", "g_in", "q_in", "qc_in", "k_in", "kd_in", "m_in"))
        pz_ready = sem("pz_ready")
        gate_ready = sem("gate_ready")
        ring_full = sem("ring_full")
        u_full, u_free = sem("u_full"), sem("u_free")
        g_full, g_free = sem("g_full"), sem("g_free")
        s_full, s_free = sem("s_full"), sem("s_free")
        c_full, c_free = sem("c_full"), sem("c_free")
        hid_ready, prob_ready = sem("hid_ready"), sem("prob_ready")
        halves_added = sem("halves_added")
        residual_ready, y_out = sem("residual_ready"), sem("y_out")
        dve_done, act_done, pool_done = sem("dve_done"), sem("act_done"), sem("pool_done")

        x_rows = x.rearrange("(b t p) d -> b p t d", p=P, t=NT)
        out_rows = out.rearrange("(b t p) d -> b p t d", p=P, t=NT)

        N_MADE = 6

        block = ctx.enter_context(nc.Block())

        @block.sync
        def _(sp):
            x_used, res_used, c_seen, ring_seen = Count(), Count(), Count(), Count()
            q_s, k_s, t_s, g_s, m_s = Count(), Count(), Count(), Count(), Count()
            counts = [x_used, res_used, c_seen, ring_seen, q_s, k_s, t_s, g_s, m_s]

            def load_x(b):
                wait(sp, xn_ready, x_used.now)
                x_used.up(NT)
                sp.dma_start(xt[:, :, :], x_rows[b]).then_inc(x_in, 16)

            def restack_t():
                wait(sp, ring_full, ring_seen.now)
                sp.wait_ge(t_split, t_s.up())
                for s, (part, _) in enumerate(TERMS):
                    sp.dma_start(t_st[FD * s:FD * (s + 1), :, :], t_parts[:, part, :]).then_inc(t_in, 16)

            def stack_q(stacked, done):
                for s, (part, _) in enumerate(TERMS):
                    sp.dma_start(stacked[2 * AD * s:2 * AD * (s + 1), :, :], q_parts[:, part, :]).then_inc(done, 16)

            def stack_k(ab):
                for s, (_, part) in enumerate(TERMS):
                    r = AD * (2 * s + ab)
                    sp.dma_start(k_st[r:r + AD, ab, :, :],
                                 k_parts[HALF * ab:HALF * (ab + 1), part, :]).then_inc(k_in, 16)

            def restack_chunks():
                sp.wait_ge(q_split, q_s.up())
                stack_q(q_ch, qc_in)
                restack_g()
                sp.wait_ge(k_split, k_s.up())
                stack_k(0)
                stack_k(1)

            def restack_g():
                sp.wait_ge(g_split, g_s.up())
                for part in range(3):
                    sp.dma_start(g_st[2 * NE * part:2 * NE * (part + 1), :, :], g_parts[:, part, :]).then_inc(g_in, 16)

            def restack_q(scores):
                wait(sp, ring_full, ring_seen.up(scores))
                stack_q(q_st, q_in)
                sp.wait_ge(k_turn, k_s.now)
                for ab in range(2):
                    for s, (_, part) in enumerate(TERMS):
                        r = AD * (2 * s + ab)
                        sp.dma_start(k_dg[r:r + AD, :, N * ab:N * (ab + 1)],
                                     k_turned[HALF * ab:HALF * (ab + 1), part, :]).then_inc(kd_in, 16)

            def place_max():
                for h in range(2):
                    sp.wait_ge(m_split, m_s.up())
                    for ab in range(2):
                        for part in range(3):
                            r = QK_ROWS + 3 * ab + part
                            sp.dma_start(q_st[r:r + 1, 4 * h:4 * h + 4, :],
                                         m_parts[:, h, part, HALF * ab:HALF * (ab + 1)]).then_inc(m_in, 16)
                ring_seen.up(GROUPS)

            def store(b, before):
                sp.wait_ge(c_free, c_seen.up(OUT_C + before))
                sp.dma_start(out_rows[b], y[:, :, :]).then_inc(y_out, 16)

            def prologue():
                load_x(0)
                sp.dma_start(first_sb[:, :], first).then_inc(first_in, 16)
                sp.dma_start(w1raw, w1b1).then_inc(w1raw_in, 16)
                sp.dma_start(rows_sb[:, :], rows.broadcast_to([P, NT * FH * NE + D])).then_inc(rows_in, 16)
                sp.dma_start(weights_sb[:, :], weights).then_inc(const_in, 16)
                sp.dma_start(gate_spread[:, :, :], gate_spread_d).then_inc(const_in, 16)
                sp.dma_start(bo_two, biases.broadcast_to([P, 2 * D])).then_inc(const_in, 16)
                load_x(1)
                sp.wait_ge(w1_split, 1)
                for s, (_, part) in enumerate(TERMS):
                    sp.dma_start(w1_st[FD * s:FD * (s + 1), :], w1parts[0:FD, part, :]).then_inc(w1_in, 16)
                for part in range(3):
                    r = FFN_ROWS + part
                    sp.dma_start(w1_st[r:r + 1, :], w1parts[FD:FD + 1, part, :]).then_inc(w1_in, 16)
                restack_t()
                sp.wait_ge(made, N_MADE)
                for ab in range(2):
                    r = QK_ROWS + 3 * ab
                    sp.dma_start(k_dg[r:r + 3, :, N * ab:N * (ab + 1)], minus_d).then_inc(w1_in, 16)
                restack_chunks()
                restack_q(0)
                place_max()
                c_seen.up(3 + CHUNK_C + 3)

            def body(b, more, more2):
                if more2:
                    load_x(b + 2)
                wait(sp, residual_ready, res_used.now)
                res_used.up()
                sp.dma_start(xr[:, :, :], x_rows[b]).then_inc(xr_in, 16)
                if more:
                    restack_t()
                    restack_chunks()
                    restack_q(2 * NG)
                c_seen.up(SUM_C)
                store(b, BEFORE_OUT_C if more else 0)
                if more:
                    place_max()
                    c_seen.up(CHUNK_C - BEFORE_OUT_C + (3 if more2 else 0))

            over_batches(sp, counts, prologue, body)
            sp.wait_ge(y_out, 16 * B)

        @block.gpsimd
        def _(pool):
            step = Count()
            var_s, q_s, k_s, xr_s, q_in_s, k_in_s, c_s, kd_in_s, u_s, y_s, qc_in_s, t_s, t_in_s = (Count() for _ in range(13))
            counts = [step, var_s, q_s, k_s, xr_s, q_in_s, k_in_s, c_s, kd_in_s, u_s, y_s, qc_in_s,
                      t_s, t_in_s]

            def link(ins):
                ins.then_inc(pool_done, 1)
                pool.wait_ge(pool_done, step.up())

            def power():
                pool.wait_ge(var_ready, var_s.up())
                nc.gpsimd.tensor_tensor(rstd[:, :], var_eps[:, :], minus_half[:, :], ALU.pow).then_inc(rstd_ready, 1)

            zeros = zero_col[:, :].broadcast_to([P, N])

            def split(src, parts, done):
                link(nc.gpsimd.tensor_tensor(parts[:, 0, :], src, zeros, ALU.add))
                link(nc.gpsimd.tensor_tensor(qk_tmp[:, :], src, parts[:, 0, :], ALU.subtract))
                link(nc.gpsimd.tensor_tensor(parts[:, 1, :], qk_tmp[:, :], zeros, ALU.add))
                nc.gpsimd.tensor_tensor(parts[:, 2, :], qk_tmp[:, :], parts[:, 1, :], ALU.subtract).then_inc(done, 1)

            def split_t():
                wait(pool, t_in, t_in_s.now)
                t_in_s.up(16 * len(TERMS))
                pool.wait_ge(c_free, c_s.up())
                split(t32[:, :], t_parts, t_split)
                pool.wait_ge(t_split, t_s.up())

            def split_q():
                wait(pool, q_in, q_in_s.now)
                q_in_s.up(Q_DMAS * 16)
                wait(pool, qc_in, qc_in_s.now)
                qc_in_s.up(Q_DMAS * 16)
                pool.wait_ge(c_free, c_s.up())
                split(q32[:, :], q_parts, q_split)

            def split_k():
                pool.wait_ge(q_split, q_s.up())
                wait(pool, k_in, k_in_s.now)
                k_in_s.up(K_DMAS * 16)
                pool.wait_ge(c_free, c_s.up())
                split(k32[:, :], k_parts, k_split)
                pool.wait_ge(k_split, k_s.up())
                wait(pool, kd_in, kd_in_s.now)
                kd_in_s.up(K_DMAS * 16)
                for part in range(3):
                    ins = nc.gpsimd.tensor_tensor(
                        k_turned[:, part, :].rearrange("p (k m) -> p m k", m=NBK),
                        k_parts[:, part, :].rearrange("p (m k) -> p m k", m=NBK),
                        zero_col[:, :].unsqueeze(2).broadcast_to([P, NBK, BZ]), ALU.add)
                ins.then_inc(k_turn, 1)

            def add_halves(j):
                pool.wait_ge(u_free, u_s.up(2))
                nc.gpsimd.tensor_tensor(gated[:, 2 * j, :], gated[:, 2 * j, :], gated[:, 2 * j + 1, :],
                                        ALU.add).then_inc(halves_added, 1)

            def gelu_phase(early):
                for j in range(FH - 1):
                    add_halves(j)
                    if early and j == 1:
                        power()
                c_s.up(CHUNK_C)

            def prologue():
                nc.gpsimd.memset(zero_col[:, :], 0.0)
                link(nc.gpsimd.memset(minus_half[:, :], -0.5))
                nc.gpsimd.memset(k_dg[:, :, :].bitcast(U32), 0).then_inc(made, 1)
                power()
                nc.gpsimd.memset(k_st[:, :, :, :].bitcast(U32), 0).then_inc(made, 1)
                pool.wait_ge(const_in, 16 * 3)
                nc.gpsimd.tensor_tensor(bo_sb[:, :], bo_two[:, 0:D], bo_two[:, D:2 * D], ALU.add).then_inc(made, 1)
                pool.wait_ge(made, N_MADE)
                split_t()
                split_q()
                split_k()
                gelu_phase(True)

            def body(b, more, more2):
                if more:
                    split_t()
                add_halves(FH - 1)
                if more:
                    split_q()
                    split_k()
                pool.wait_ge(xr_in, xr_s.up(16))
                wait(pool, y_out, y_s.now)
                y_s.up(16)
                for j in range(NT):
                    ins = nc.gpsimd.tensor_tensor(y[:, j, :], xr[:, j, :], bo_sb[:, :], ALU.add)
                ins.then_inc(residual_ready, 1)
                if more:
                    c_s.up(SUM_C + OUT_C)
                    u_s.up()
                    gelu_phase(more2)

            over_batches(pool, counts, prologue, body)

        @block.scalar
        def _(act):
            ring_s, l2_s, g_s, s_s, c_s = (Count() for _ in range(5))
            counts = [ring_s, l2_s, g_s, s_s, c_s]

            def take_xnT():
                act.wait_ge(s_full, s_s.up())
                nc.scalar.activation(xnT[:, :], s_bank[:, :], ACT.Identity).then_inc(s_free, 1)

            def gate_exp():
                act.wait_ge(s_free, s_s.up())
                nc.scalar.activation(pz[:, :], z[:, :], ACT.Exp).then_inc(pz_ready, 1)

            def take_q():
                act.wait_ge(c_full, c_s.up())
                nc.scalar.activation(q32[:, :], c_bank[:, :], ACT.Identity, bias=bq_scaled[:, :],
                                     scale=SCALE).then_inc(c_free, 1)

            def take_k():
                act.wait_ge(c_full, c_s.up())
                nc.scalar.activation(k32[:, :], c_bank[:, :], ACT.Identity, bias=bias3[:, 1:2]).then_inc(c_free, 1)

            def copy_gates(n):
                act.wait_ge(g_full, g_s.up())
                if n >= 2:
                    act.wait_ge(u_free, l2_s.now + n - 1)
                nc.scalar.activation(gates[:, n % 2, :], g_bank[:, :], ACT.Identity).then_inc(g_free, 1)

            def gelu_phase(early):
                s_s.up(CHUNK_S)
                c_s.up(CHUNK_C)
                for gi in range(GROUPS):
                    act.wait_ge(ring_full, ring_s.up())
                    if gi >= G_RING and gi % 2 == 0:
                        act.wait_ge(u_full, l2_s.now + (gi - G_RING) // 2 + 1)
                    nc.scalar.activation(hid[:, gi % G_RING, :, :], ring[:, gi % 2, :, :],
                                         ACT.Gelu).then_inc(hid_ready, 1)
                    if early and gi == TURN_AT:
                        take_xnT()
                    if gi + 1 in SECOND_AT:
                        copy_gates(SECOND_AT.index(gi + 1))
                    if early and gi == Q_AT:
                        c_s.up()
                        take_q()
                l2_s.up(2 * FH)
                s_s.up()

            def prologue():
                act.wait_ge(first_in, 16)
                nc.scalar.mul(bq_scaled[:, :], bias3[:, 0:1], SCALE).then_inc(act_done, 1)
                act.wait_ge(act_done, 1)
                take_xnT()
                gate_exp()
                s_s.up(GATES_S)
                c_s.up()
                take_q()
                take_k()
                gelu_phase(True)

            def body(b, more, more2):
                for g in range(NG):
                    for n in range(2):
                        act.wait_ge(ring_full, ring_s.up())
                        at = n * UNIT_WIDTH[0]
                        src = ring[:, n, :, :].rearrange("p a n -> p (a n)")[:, 0:UNIT_WIDTH[n]]
                        nc.scalar.activation(prob_half[g // 4][:, g % 4, at:at + UNIT_WIDTH[n]], src,
                                             ACT.Exp).then_inc(prob_ready, 1)
                        if more and (g, n) == (0, 0):
                            take_k()
                    if more and g == 1:
                        gate_exp()
                    if g == 4:
                        act.wait_ge(c_full, c_s.up())
                        nc.scalar.activation(combT[:, :], c_bank[:, :], ACT.Identity).then_inc(c_free, 1)
                if more:
                    s_s.up(GATES_S + OUT_S)
                    c_s.up(OUT_C)
                    l2_s.up()
                    g_s.up()
                    gelu_phase(more2)

            over_batches(act, counts, prologue, body)

        @block.vector
        def _(dve):
            step = Count()
            x_s, r_s, sf, cf, uf, gf, pz_s = (Count() for _ in range(7))
            m_s, g_s, g_in_s, m_in_s, res_s = (Count() for _ in range(5))
            counts = [step, x_s, r_s, sf, cf, uf, gf, pz_s, m_s, g_s, g_in_s, m_in_s, res_s]

            def link(ins):
                ins.then_inc(dve_done, 1)
                dve.wait_ge(dve_done, step.up())

            def split(src, parts, tmp, done):
                link(nc.vector.tensor_copy(parts[:, 0, :], src))
                link(nc.vector.tensor_tensor(tmp, src, parts[:, 0, :], ALU.subtract))
                link(nc.vector.tensor_copy(parts[:, 1, :], tmp))
                nc.vector.tensor_tensor(parts[:, 2, :], tmp, parts[:, 1, :], ALU.subtract).then_inc(done, 1)

            def norm_stats(j):
                if j == 0:
                    dve.wait_ge(x_in, x_s.up(16))
                ins = nc.vector.bn_stats(stats[:, j, :], xt[:, j, :])
                if j < NT - 1:
                    return
                link(ins)
                nc.vector.tensor_copy(idle[:, :], stats[:, 0, 0:1])
                for j in range(NT):
                    ins = nc.vector.bn_aggr(mean_var[:, j, :], stats[:, j, :])
                link(ins)
                nc.vector.tensor_scalar(var_eps[:, :], mean_var[:, :, 1], EPS, None, ALU.add).then_inc(var_ready, 1)

            def normalise(j):
                if j == 0:
                    dve.wait_ge(rstd_ready, r_s.up())
                nc.vector.tensor_scalar(xn[:, j, :], xt[:, j, :], mean_var[:, j, 0:1], rstd[:, j:j + 1],
                                        ALU.subtract, ALU.mult).then_inc(xn_ready, 1)

            def take_t():
                dve.wait_ge(c_full, cf.up())
                nc.vector.tensor_scalar(t32[:, :], c_bank[:, :], bias3[:, 2:3], None, ALU.add).then_inc(c_free, 1)

            R = NT * FH // 4

            def by_expert(t):
                return t[:, :].rearrange("p (r e h) -> p r h e", r=R, h=4)

            def per_head(k, spread=True):
                v = top[:, k, :].rearrange("p (r h) -> p r h", h=4)
                return v.unsqueeze(3).broadcast_to([P, R, 4, NE]) if spread else v

            def take_logits():
                dve.wait_ge(s_full, sf.up())
                zp = s_bank[:, :].rearrange("p (r e h) -> p r h e", r=R, h=4)
                link(nc.vector.tensor_reduce(per_head(0, False), zp, AX.X, ALU.max))
                nc.vector.tensor_tensor(by_expert(z), zp, per_head(0), ALU.subtract).then_inc(s_free, 1)

            def route():
                dve.wait_ge(s_free, sf.now)
                for n, one in enumerate([one1, one2]):
                    if n == 0:
                        link(nc.vector.scalar_tensor_tensor(c1[:, :], z[:, :], 0.0, rank[:, :], ALU.is_equal, ALU.mult))
                    else:
                        link(nc.vector.scalar_tensor_tensor(z2[:, :], one1[:, :], -BIG, z[:, :], ALU.mult, ALU.add))
                        link(nc.vector.tensor_reduce(per_head(1, False), by_expert(z2), AX.X, ALU.max))
                        link(nc.vector.tensor_tensor(by_expert(one2), by_expert(z2), per_head(1), ALU.is_equal))
                        link(nc.vector.tensor_tensor(c1[:, :], one2[:, :], rank[:, :], ALU.mult))
                    link(nc.vector.tensor_reduce(per_head(2 + n, False), by_expert(c1), AX.X, ALU.max))
                    link(nc.vector.tensor_tensor(by_expert(one), by_expert(c1), per_head(2 + n), ALU.is_equal))
                link(nc.vector.tensor_tensor(c1[:, :], one1[:, :], one2[:, :], ALU.add))
                dve.wait_ge(pz_ready, pz_s.up())
                link(nc.vector.tensor_reduce(per_head(4, False), by_expert(pz), AX.X, ALU.add))
                link(nc.vector.reciprocal(top[:, 5, :], top[:, 4, :]))
                link(nc.vector.tensor_tensor(z2[:, :], pz[:, :], c1[:, :], ALU.mult))
                nc.vector.tensor_tensor(by_expert(c1), by_expert(z2), per_head(5), ALU.mult).then_inc(gate_ready, 1)

            def take_gates():
                dve.wait_ge(s_full, sf.up())
                wait(dve, g_in, g_in_s.now)
                g_in_s.up(16 * 3)
                split(s_bank[:, :], g_parts, dve_tmp[:, :], g_split)
                dve.wait_ge(g_split, g_s.up())
                nc.vector.tensor_copy(gT32[:, :], s_bank[:, :]).then_inc(s_free, 1)

            def take_v():
                dve.wait_ge(s_full, sf.up())
                for ab in range(2):
                    rows = slice(HALF * ab, HALF * (ab + 1))
                    src = s_bank[rows, :].rearrange("p (m g d) -> p m g d", m=NBK, d=AD)
                    bias = bv_sb[rows, HALF * ab:HALF * (ab + 1)].rearrange("p (g d) -> p g d", d=AD)
                    ins = nc.vector.tensor_tensor(v_dg[rows, :, :, 16 * ab:16 * ab + AD], src,
                                                  bias.unsqueeze(1).broadcast_to([HALF, NBK, NG, AD]), ALU.add)
                ins.then_inc(s_free, 1)

            def take_max(g, c):
                bank, full, free, cnt = ((s_bank, s_full, s_free, sf), (c_bank, c_full, c_free, cf))[c % 2]
                dve.wait_ge(full, cnt.up())
                for i, col, n, width in REDUCES[c]:
                    at = g % 4 * NBK + i
                    ins = nc.vector.tensor_reduce(mx[g // 4][:, at:at + n],
                                                  bank[:, col:col + n * width].rearrange("p (n w) -> p n w", n=n),
                                                  AX.X, ALU.max)
                ins.then_inc(free, 1)

            def take_mT(h):
                rows = slice(0, MXR)
                dve.wait_ge(s_full, sf.up())
                wait(dve, m_in, m_in_s.now)
                m_in_s.up(16 * 6)
                src, parts = s_bank[rows, 0:P], m_parts[:, h, :, :]
                link(nc.vector.tensor_copy(parts[:, 0, :], src))
                link(nc.vector.tensor_tensor(m_tmp[:, :], src, parts[:, 0, :], ALU.subtract))
                nc.vector.tensor_copy(parts[:, 1, :], m_tmp[:, :]).then_inc(s_free, 1)
                dve.wait_ge(s_free, sf.now)
                nc.vector.tensor_tensor(parts[:, 2, :], m_tmp[:, :], parts[:, 1, :], ALU.subtract).then_inc(m_split, 1)
                dve.wait_ge(m_split, m_s.up())

            def gate_half(n):
                dve.wait_ge(g_free, gf.up())
                dve.wait_ge(u_full, uf.up())
                nc.vector.tensor_tensor(gated[:, n, :], u_bank[:, :], gates[:, n % 2, :], ALU.mult).then_inc(u_free, 1)

            def take_o(grp):
                bank, full, free = ((u_bank, u_full, u_free), (g_bank, g_full, g_free))[grp]
                dve.wait_ge(full, uf.up() if grp == 0 else gf.now)
                nc.vector.tensor_copy(o_sb[:, grp, :], bank[:, :]).then_inc(free, 1)

            def normalise_o(grp):
                bank, full, free, cnt = ((c_bank, c_full, c_free, cf), (s_bank, s_full, s_free, sf))[grp]
                dve.wait_ge(full, cnt.up())
                heads = bank[:, :].rearrange("p (j k r) -> p j k r", j=NT, r=16)
                recip = rden[:, grp, :].rearrange("p (j k) -> p j k", j=NT)
                link(nc.vector.reciprocal(recip, heads[:, :, :, AD]))
                nc.vector.tensor_tensor(o_tok[:, :, HALF * grp:HALF * (grp + 1)].rearrange("p j (k d) -> p j k d", d=AD),
                                        heads[:, :, :, 0:AD], recip.unsqueeze(3).broadcast_to([P, NT, 8, AD]),
                                        ALU.mult).then_inc(free, 1)

            def take_oT():
                dve.wait_ge(c_full, cf.up())
                nc.vector.tensor_copy(oT[:, :], c_bank[:, :]).then_inc(c_free, 1)

            def finish():
                dve.wait_ge(residual_ready, res_s.up())
                dve.wait_ge(c_full, cf.up())
                row = y[:, :, :].rearrange("p t d -> p (t d)")
                nc.vector.tensor_tensor(row, c_bank[:, :], row, ALU.add).then_inc(c_free, 1)

            def gelu_phase(with_out, early):
                for gi in range(GROUPS):
                    if with_out and gi == 1:
                        normalise_o(0)
                    if gi == VALUES_AT:
                        if with_out:
                            take_o(1)
                        take_v()
                    if with_out and gi == TURN_O_AT:
                        normalise_o(1)
                    if gi in MAX_AT:
                        take_mT(MAX_AT.index(gi))
                    if early and 0 <= gi - STATS_AT < NT:
                        norm_stats(gi - STATS_AT)
                    if early and 0 <= gi - NORM_AT < NT:
                        normalise(gi - NORM_AT)
                    if early and gi == TURN_AT:
                        sf.up()
                    first, rest = chunks_at(gi)
                    for chunk in first:
                        take_max(chunk // 4, chunk % 4)
                    if gi in SECOND_AT:
                        gate_half(SECOND_AT.index(gi))
                    if with_out and gi == TURN_BACK_AT:
                        take_oT()
                    if with_out and gi == OUT_AT:
                        finish()
                    for chunk in rest:
                        take_max(chunk // 4, chunk % 4)
                    if early and gi == T_AT:
                        take_t()

            def prologue():
                nc.vector.memset(t_st[FFN_ROWS:, :, :], 1.0).then_inc(made, 1)
                for j in range(NT):
                    norm_stats(j)
                nc.vector.memset(v_dg[:, :, :, :], 0.0)
                for j in range(NT):
                    normalise(j)
                dve.wait_ge(w1raw_in, 16)
                split(w1raw, w1parts, w1tmp, w1_split)
                sf.up()
                take_t()
                nc.vector.memset(mx[0][:, :], 0.0)
                link(nc.vector.memset(mx[1][:, :], 0.0))
                for ab in range(2):
                    rows = slice(HALF * ab, HALF * (ab + 1))
                    nc.vector.memset(v_dg[rows, :, :, 16 * ab + AD:16 * ab + AD + 1], 1.0).then_inc(made, 1)
                take_logits()
                dve.wait_ge(rows_in, 16)
                route()
                take_gates()
                cf.up(2)
                gelu_phase(False, True)

            def body(b, more, more2):
                if more:
                    take_logits()
                gate_half(2 * FH - 1)
                if more:
                    route()
                    cf.up(2)
                cf.up()
                if more:
                    take_gates()
                take_o(0)
                if more:
                    gf.up()
                    gelu_phase(True, more2)
                else:
                    gf.up()
                    normalise_o(0)
                    take_o(1)
                    normalise_o(1)
                    take_oT()
                    finish()

            over_batches(dve, counts, prologue, body)

        @block.tensor
        def _(pe):
            mm = nc.tensor.matmul
            xnT_at, t_at, o1_at, half_at, o_at = [None], [None], [None], [None], [None, None]
            xn_s, s_uses, c_uses, u_uses, g_uses = (Count() for _ in range(5))
            gate_s, hid_s, prob_s, added_s, t_in_s, g_in_s, q_s, qc_s, k_s, m_s, kd_s = (Count() for _ in range(11))
            counts = [xn_s, s_uses, c_uses, u_uses, g_uses, gate_s, hid_s, prob_s, added_s, t_in_s, g_in_s,
                      q_s, qc_s, k_s, m_s, kd_s]

            def claim(free, uses):
                wait(pe, free, uses.now)
                uses.up()

            def turn_xn():
                pe.wait_ge(xn_ready, xn_s.up(NT))
                claim(s_free, s_uses)
                for j in range(NT):
                    ins = nc.tensor.transpose(s_bank[:, j * P:(j + 1) * P], xn[:, j, :], ident[:, :])
                ins.then_inc(s_full, 1)
                xnT_at[0] = s_uses.now

            def project_t():
                pe.wait_ge(s_free, xnT_at[0])
                project(wm_sb, c_bank, c_free, c_uses, c_full)
                t_at[0] = c_uses.now

            def project(weight, bank, free, uses, full):
                claim(free, uses)
                mm(bank[:, :], weight[:, :], xnT[:, :], start=True, stop=True).then_inc(full, 1)

            def logits():
                pe.wait_ge(c_free, t_at[0])
                claim(s_free, s_uses)
                for j in range(NT):
                    ins = mm(s_bank[:, j * P:(j + 1) * P], t32[:, j * P:(j + 1) * P], emb_sb[:, :], start=True, stop=True)
                ins.then_inc(s_full, 1)

            def turn_gates():
                pe.wait_ge(gate_ready, gate_s.up())
                claim(s_free, s_uses)
                for j in range(NT):
                    ins = nc.tensor.transpose(s_bank[:, j * P:(j + 1) * P], c1[:, j * P:(j + 1) * P], ident[:, :])
                ins.then_inc(s_full, 1)

            def values():
                claim(s_free, s_uses)
                for m in range(NBK):
                    for ab in range(2):
                        ins = mm(s_bank[HALF * ab:HALF * (ab + 1), m * HALF:(m + 1) * HALF],
                                 xnT[:, m * BZ:(m + 1) * BZ], wv_sb[:, HALF * ab:HALF * (ab + 1)], start=True, stop=True)
                ins.then_inc(s_full, 1)

            def score_chunk(g, c):
                bank, full, free, uses = ((s_bank, s_full, s_free, s_uses), (c_bank, c_full, c_free, c_uses))[c % 2]
                claim(free, uses)
                for i, col in CHUNKS[c]:
                    lo, hi = key_range(i)
                    for ab in range(2):
                        ins = mm(bank[HALF * ab:HALF * (ab + 1), col:col + hi - lo],
                                 q_ch[:, g, i * BZ:(i + 1) * BZ], k_st[:, ab, g, lo:hi], start=True, stop=True)
                ins.then_inc(full, 1)
                if c == 3 and g % 4 == 3:
                    half_at[0] = c_uses.now

            def turn_max(h):
                pe.wait_ge(c_free, half_at[0])
                claim(s_free, s_uses)
                nc.tensor.transpose(s_bank[:, 0:P], mx[h][:, :], ident[:, :]).then_inc(s_full, 1)

            def hidden(gi):
                h = HEAD_ORDER[gi // 4]
                for a in range(2):
                    t = 2 * (gi % 4) + a
                    ins = mm(ring[:, gi % 2, a, :], w1_st[:, t * P:(t + 1) * P], t_st[:, h, :], start=True, stop=True)
                ins.then_inc(ring_full, 1)

            def spread_gates(n):
                h, u = HEAD_ORDER[n // 2], n % 2
                claim(g_free, g_uses)
                mm(g_bank[:, :], gate_spread[:, 2 * (h % 2) + u, :], g_st[:, h // 2, :],
                   start=True, stop=True).then_inc(g_full, 1)

            def second(n):
                claim(u_free, u_uses)
                pe.wait_ge(hid_ready, hid_s.now + 2 * (n + 1))
                for a in range(4):
                    t = 4 * (n % 2) + a
                    slot = (2 * n + a // 2) % G_RING
                    ins = mm(u_bank[32 * a:32 * (a + 1), :], w2_sb[:, t, :], hid[:, slot, a % 2, :], start=True, stop=True)
                ins.then_inc(u_full, 1)

            def combine_bias():
                claim(c_free, c_uses)
                mm(c_bank[:, :], b2_sb[:, :], gT32[:, :], start=True, stop=False, skip_group_check=True)

            def combine(group):
                pe.wait_ge(halves_added, added_s.up(FH // 2))
                for q in range(4):
                    ins = mm(c_bank[32 * q:32 * (q + 1), :], head_sum[:, group, :], gated[:, 8 * group + 2 * q, :],
                             start=False, stop=(group == 1), skip_group_check=True)
                if group == 1:
                    ins.then_inc(c_full, 1)

            def shifted(g, n):
                for m, col in UNITS[n]:
                    for lo, width in query_runs(m):
                        bank, c0 = col // N, col % N
                        ins = mm(ring[:, n, bank, c0:c0 + width], k_dg[:, g, m:2 * N:NBK], q_st[:, g, lo:lo + width],
                                 start=True, stop=True)
                        col += width
                ins.then_inc(ring_full, 1)

            def attend(grp, ms):
                if 0 in ms:
                    claim((u_free, g_free)[grp], (u_uses, g_uses)[grp])
                bank = (u_bank, g_bank)[grp]
                for m in ms:
                    for lo, width in query_runs(m):
                        n = next(k for k in range(2) if m in [a for a, _ in UNITS[k]])
                        col = dict(UNITS[n])[m] + n * UNIT_WIDTH[0]
                        off = 0 if lo == 0 else BZ
                        for q in range(4):
                            ins = mm(bank[32 * q:32 * (q + 1), lo:lo + width], v_dg[:, m, 4 * grp + q, :],
                                     prob_half[grp][:, q, col + off:col + off + width],
                                     start=(m == 0), stop=(m == NBK - 1), skip_group_check=True)
                if NBK - 1 in ms:
                    ins.then_inc((u_full, g_full)[grp], 1)
                    o_at[grp] = (u_uses, g_uses)[grp].now

            def turn_o(grp):
                bank, full, free, uses = ((c_bank, c_full, c_free, c_uses), (s_bank, s_full, s_free, s_uses))[grp]
                claim(free, uses)
                pe.wait_ge((u_free, g_free)[grp], o_at[grp])
                for j in range(NT):
                    ins = nc.tensor.transpose(bank[:, j * P:(j + 1) * P], o_sb[:, grp, j * P:(j + 1) * P], ident[:, :])
                ins.then_inc(full, 1)
                if grp == 1:
                    o1_at[0] = s_uses.now

            def turn_back():
                pe.wait_ge(s_free, o1_at[0])
                claim(c_free, c_uses)
                for j in range(NT):
                    ins = nc.tensor.transpose(c_bank[:, j * P:(j + 1) * P], o_tok[:, j, :], ident[:, :])
                ins.then_inc(c_full, 1)

            def project_out():
                claim(c_free, c_uses)
                for j in range(NT):
                    tok = slice(j * P, (j + 1) * P)
                    mm(c_bank[:, tok], combT[:, tok], wof_sb[:, :], start=True, stop=False)
                    ins = mm(c_bank[:, tok], oT[:, tok], woa_sb[:, :], start=False, stop=True)
                ins.then_inc(c_full, 1)

            def gelu_phase(with_out, early):
                for gi in range(GROUPS):
                    if gi == 0:
                        pe.wait_ge(t_in, t_in_s.up(16 * len(TERMS)))
                    if gi >= 2:
                        pe.wait_ge(hid_ready, hid_s.now + gi - 1)
                    elif with_out:
                        pe.wait_ge(prob_ready, prob_s.now + gi - 1)
                    hidden(gi)
                    if gi in MAX_AT:
                        turn_max(MAX_AT.index(gi))
                    if with_out:
                        if gi < 3:
                            attend(1, range(NBK)[3 * gi:3 * gi + 3])
                        if gi == 1:
                            turn_o(0)
                    if gi == VALUES_AT:
                        values()
                    if gi == SECOND_AT[0] - 1:
                        pe.wait_ge(g_in, g_in_s.up(16 * 3))
                    if gi == FIRST_CHUNK:
                        pe.wait_ge(qc_in, qc_s.up(16 * Q_DMAS))
                        pe.wait_ge(k_in, k_s.up(16 * K_DMAS))
                    if early and gi == TURN_AT:
                        turn_xn()
                    first, rest = chunks_at(gi)
                    for chunk in first:
                        score_chunk(chunk // 4, chunk % 4)
                    if early and gi == Q_AT:
                        project(wq_sb, c_bank, c_free, c_uses, c_full)
                    if gi in SECOND_AT:
                        second(SECOND_AT.index(gi))
                    if gi + 1 in SECOND_AT:
                        spread_gates(SECOND_AT.index(gi + 1))
                    if with_out and gi == TURN_O_AT:
                        turn_o(1)
                    if with_out and gi == TURN_BACK_AT:
                        turn_back()
                    if with_out and gi == OUT_AT:
                        project_out()
                    for chunk in rest:
                        score_chunk(chunk // 4, chunk % 4)
                    if early and gi == T_AT:
                        project_t()

            def prologue():
                pe.wait_ge(first_in, 16)
                turn_xn()
                project_t()
                logits()
                pe.wait_ge(const_in, 16 * 3)
                project(wq_sb, c_bank, c_free, c_uses, c_full)
                project(wk_sb, c_bank, c_free, c_uses, c_full)
                pe.wait_ge(made, N_MADE)
                turn_gates()
                pe.wait_ge(w1_in, 16 * 11)
                gelu_phase(False, True)

            def body(b, more, more2):
                if more:
                    logits()
                pe.wait_ge(q_in, q_s.up(16 * Q_DMAS))
                pe.wait_ge(kd_in, kd_s.up(16 * K_DMAS))
                for g in range(NG):
                    if g % 4 == 0:
                        pe.wait_ge(m_in, m_s.up(16 * 6))
                    for n in range(2):
                        if g == 0:
                            pe.wait_ge(hid_ready, hid_s.now + GROUPS + n - 1)
                        else:
                            pe.wait_ge(prob_ready, prob_s.now + 2 * g + n - 1)
                        shifted(g, n)
                        if more and (g, n) == (0, 0):
                            project(wk_sb, c_bank, c_free, c_uses, c_full)
                    if g == 0:
                        second(2 * FH - 1)
                        hid_s.up(GROUPS)
                    if g == 1:
                        combine_bias()
                    if g in (2, 3):
                        combine(g - 2)
                    if g >= 4:
                        if g == 4:
                            pe.wait_ge(prob_ready, prob_s.now + 8)
                        attend(0, [2 * (g - 4), 2 * (g - 4) + 1])
                    if more and g == 5:
                        turn_gates()
                prob_s.up(2 * NG)
                if more:
                    gelu_phase(True, more2)
                else:
                    pe.wait_ge(prob_ready, prob_s.now)
                    attend(1, range(NBK))
                    turn_o(0)
                    turn_o(1)
                    turn_back()
                    project_out()

            over_batches(pe, counts, prologue, body)


def kernel(**inputs):
    import ml_dtypes as _ml
    import numpy as _np
    import concourse.bacc as _bacc
    from concourse import mybir as _mybir
    from concourse.bass_utils import run_bass_kernel_spmd as _run

    a = {k: _np.asarray(v) for k, v in inputs.items()}
    f32 = _np.float32

    def cols(*parts):
        return _np.concatenate([p.reshape(P, -1) for p in parts], axis=1)

    def pair_cols(w):
        return w.reshape(-1, NG, 2, AD).transpose(0, 2, 3, 1).reshape(-1, D)

    wv = a["L0_attn_Wv"].reshape(D, NG, 2, AD).transpose(0, 2, 1, 3).reshape(D, D)
    bv = a["L0_attn_bv"].reshape(NG, 2, AD).transpose(1, 0, 2).reshape(D)
    wm = a["L0_ffn_Wm"].reshape(D, FH, FD).transpose(0, 2, 1).reshape(D, D)
    bm = a["L0_ffn_bm"].reshape(FH, FD).T
    emb = _np.zeros((FD, FH // 2, 2, 2, NE, FH // 2), f32)
    b2 = _np.zeros((2, NE, FH // 2, FH // 2, 2, FD), f32)
    for hp in range(FH // 2):
        for ab in range(2):
            emb[:, hp, ab, ab, :, hp] = a["L0_ffn_expert_emb"]
            b2[ab, :, hp, hp, ab, :] = a["L0_ffn_b2"]
    w1b1 = _np.concatenate([a["L0_ffn_W1"].transpose(1, 0, 2).reshape(FD, NE * HID),
                            a["L0_ffn_b1"].reshape(1, NE * HID)])
    w2 = _np.zeros((2, HID, NTILE, 2, FD), f32)
    for k in range(2):
        w2[k, :, :, k, :] = a["L0_ffn_W2"].reshape(NTILE, 2, HID, FD)[:, k].transpose(1, 0, 2)
    gate_spread = _np.zeros((3, 2, NE, 2, 2, NE // 2, FD), _ml.bfloat16)
    for ab in range(2):
        for e in range(NE):
            gate_spread[:, ab, e, ab, e // 8, e % 8, :] = 1
    head_sum = _np.zeros((NE // 2, FD, 2, 2, FD), f32)
    for o in range(FD):
        for ab in range(2):
            head_sum[:, o, ab, ab, o] = 1
    arrays = {
        "x": a["L0_attn_x"].reshape(B * N, D),
        "first": cols(_np.eye(P, dtype=f32), wm, emb, pair_cols(a["L0_attn_bq"]), pair_cols(a["L0_attn_bk"]), bm),
        "weights": cols(pair_cols(a["L0_attn_Wq"]), pair_cols(a["L0_attn_Wk"]), wv, a["L0_attn_Wo"], a["L0_ffn_Wo"],
                        b2, w2, head_sum),
        "rows": _np.concatenate([_np.tile(_np.repeat(_np.arange(NE, 0, -1, dtype=f32), FH // 2), 2 * NT),
                                 bv]).reshape(1, -1),
        "biases": _np.concatenate([a["L0_attn_bo"], a["L0_ffn_bo"]]).reshape(1, -1),
        "w1b1": w1b1, "gate_spread": gate_spread.reshape(GATE_ROWS, 4, P),
        "minus": _np.full((3, NG * N), -1, _ml.bfloat16),
    }
    nc = _bacc.Bacc("TRN2", target_bir_lowering=False, num_devices=1)
    feed, args = {}, []
    for name, v in arrays.items():
        v = _np.ascontiguousarray(v)
        feed[f"in_{name}"] = v
        args.append(nc.dram_tensor(f"in_{name}", v.shape, _mybir.dt.from_np(v.dtype), kind="ExternalInput").ap())
    args.append(nc.dram_tensor("out_0", (B * N, D), _mybir.dt.from_np(_np.dtype("float32")), kind="ExternalOutput").ap())
    program(nc, *args)
    r = _run(nc, [feed], core_ids=[0])
    return r.results[0]["out_0"].reshape(B, N, D)
```
